# Optimizing a Trainium2 kernel written in Bass

```python
import numpy as np
import jax
import jax.numpy as jnp

def _softmax(x, axis=-1):
    return jax.nn.softmax(x, axis=axis)

def _gelu(x):
    return jax.nn.gelu(x, approximate=True)

def _silu(x):
    return jax.nn.silu(x)

def _sigmoid(x):
    return jax.nn.sigmoid(x)

def _layernorm(x, axis=-1, eps=1e-05):
    m = jnp.mean(x, axis=axis, keepdims=True)
    v = jnp.var(x, axis=axis, keepdims=True)
    return (x - m) / jnp.sqrt(v + eps)

def _scatter_add(tgt, idx, src, axis=0):
    return tgt.at[idx].add(src)

def _segment_sum(src, seg, n):
    return jax.ops.segment_sum(src, seg, n)
kernel_name = 'mk_prb_d1_jaxref_r8_7d6433'

def setup_inputs(seed: int=0):
    np.random.seed(seed)
    _w = jnp.asarray

    def _L0_attn_setup():
        import jax, jax.numpy as jnp
        import numpy as np
        import math
        D_MODEL = 128
        NUM_HEADS = 16
        HEAD_DIM = D_MODEL // NUM_HEADS
        ROPE_THETA = 10000.0

        def _rope_tables(seq_len, dim, theta=ROPE_THETA):
            inv = 1.0 / theta ** (jnp.arange(0, dim, 2, dtype=jnp.float32) / dim)
            t = jnp.arange(seq_len, dtype=jnp.float32)
            f = jnp.outer(t, inv)
            cos = jnp.repeat(jnp.cos(f), 2, axis=-1)
            sin = jnp.repeat(jnp.sin(f), 2, axis=-1)
            return (cos, sin)

        def _rotate_half(x):
            x1 = x[..., ::2]
            x2 = x[..., 1::2]
            return jnp.stack((-x2, x1), axis=-1).reshape(x.shape)
        key = jax.random.key(seed)
        ks = jax.random.split(key, 5)
        scale = 1.0 / math.sqrt(D_MODEL)
        return {'x': jax.random.normal(ks[0], (2, 256, D_MODEL), dtype=jnp.float32), 'W_Q': jax.random.normal(ks[1], (D_MODEL, D_MODEL), dtype=jnp.float32) * scale, 'W_K': jax.random.normal(ks[2], (D_MODEL, D_MODEL), dtype=jnp.float32) * scale, 'W_V': jax.random.normal(ks[3], (D_MODEL, D_MODEL), dtype=jnp.float32) * scale, 'W_O': jax.random.normal(ks[4], (D_MODEL, D_MODEL), dtype=jnp.float32) * scale}
    _L0_attn_in = _L0_attn_setup()

    def _L0_ffn_setup():
        import jax, jax.numpy as jnp
        import numpy as np
        E = 8
        TOPK = 2

        def _moe_forward(x, Wg, W1, W2, W3):
            B, S, D = x.shape
            xt = x.reshape(-1, D)
            T = xt.shape[0]
            logits = xt @ Wg.T
            scores = jax.nn.softmax(logits, axis=-1)
            w, idx = jax.lax.top_k(scores, TOPK)
            w = w / (w.sum(axis=-1, keepdims=True) + 1e-20)
            cw = jnp.zeros((T, E), xt.dtype).at[jnp.arange(T)[:, None], idx].add(w)
            h = jax.nn.silu(jnp.einsum('td,ehd->teh', xt, W1)) * jnp.einsum('td,ehd->teh', xt, W3)
            out = jnp.einsum('teh,edh->ted', h, W2)
            y = jnp.einsum('te,ted->td', cw, out)
            return y.reshape(B, S, D)
        key = jax.random.key(seed)
        k0, k1, k2, k3, k4 = jax.random.split(key, 5)
        B, S, D, H = (1, 256, 128, 352)
        scale = 0.02
        x = jax.random.normal(k0, (B, S, D), jnp.float32)
        Wg = jax.random.normal(k1, (E, D), jnp.float32) * scale
        W1 = jax.random.normal(k2, (E, H, D), jnp.float32) * scale
        W2 = jax.random.normal(k3, (E, D, H), jnp.float32) * scale
        W3 = jax.random.normal(k4, (E, H, D), jnp.float32) * scale
        return {'x': x, 'Wg': Wg, 'W1': W1, 'W2': W2, 'W3': W3}
    _L0_ffn_in = _L0_ffn_setup()
    _d = {'L0_attn_x': _L0_attn_in['x'], 'L0_attn_W_Q': _L0_attn_in['W_Q'], 'L0_attn_W_K': _L0_attn_in['W_K'], 'L0_attn_W_V': _L0_attn_in['W_V'], 'L0_attn_W_O': _L0_attn_in['W_O'], 'L0_ffn_Wg': _L0_ffn_in['Wg'], 'L0_ffn_W1': _L0_ffn_in['W1'], 'L0_ffn_W2': _L0_ffn_in['W2'], 'L0_ffn_W3': _L0_ffn_in['W3']}
    _x0 = _d['L0_attn_x']
    _d['L0_attn_x'] = jax.random.normal(jax.random.fold_in(jax.random.key(seed), 1), (8, 512, 128), dtype=_x0.dtype)
    del _x0
    return _d

def reference(L0_attn_x, L0_attn_W_Q, L0_attn_W_K, L0_attn_W_V, L0_attn_W_O, L0_ffn_Wg, L0_ffn_W1, L0_ffn_W2, L0_ffn_W3):

    def _L0_attn_ref(x, W_Q, W_K, W_V, W_O):
        import jax, jax.numpy as jnp
        import numpy as np
        import math
        D_MODEL = 128
        NUM_HEADS = 16
        HEAD_DIM = D_MODEL // NUM_HEADS
        ROPE_THETA = 10000.0

        def _rope_tables(seq_len, dim, theta=ROPE_THETA):
            inv = 1.0 / theta ** (jnp.arange(0, dim, 2, dtype=jnp.float32) / dim)
            t = jnp.arange(seq_len, dtype=jnp.float32)
            f = jnp.outer(t, inv)
            cos = jnp.repeat(jnp.cos(f), 2, axis=-1)
            sin = jnp.repeat(jnp.sin(f), 2, axis=-1)
            return (cos, sin)

        def _rotate_half(x):
            x1 = x[..., ::2]
            x2 = x[..., 1::2]
            return jnp.stack((-x2, x1), axis=-1).reshape(x.shape)
        B, L, _ = x.shape

        def proj(W):
            return jnp.einsum('bld,ed->ble', x, W).reshape(B, L, NUM_HEADS, HEAD_DIM).transpose(0, 2, 1, 3)
        q, k, v = (proj(W_Q), proj(W_K), proj(W_V))
        cos, sin = _rope_tables(L, HEAD_DIM)
        cos = cos[None, None].astype(x.dtype)
        sin = sin[None, None].astype(x.dtype)
        q = q * cos + _rotate_half(q) * sin
        k = k * cos + _rotate_half(k) * sin
        scores = jnp.einsum('bhqd,bhkd->bhqk', q, k) / math.sqrt(HEAD_DIM)
        attn = jax.nn.softmax(scores, axis=-1)
        ctx = jnp.einsum('bhqk,bhkd->bhqd', attn, v)
        ctx = ctx.transpose(0, 2, 1, 3).reshape(B, L, D_MODEL)
        return jnp.einsum('bld,ed->ble', ctx, W_O)

    def _L0_ffn_ref(x, Wg, W1, W2, W3):
        import jax, jax.numpy as jnp
        import numpy as np
        E = 8
        TOPK = 2

        def _moe_forward(x, Wg, W1, W2, W3):
            B, S, D = x.shape
            xt = x.reshape(-1, D)
            T = xt.shape[0]
            logits = xt @ Wg.T
            scores = jax.nn.softmax(logits, axis=-1)
            w, idx = jax.lax.top_k(scores, TOPK)
            w = w / (w.sum(axis=-1, keepdims=True) + 1e-20)
            cw = jnp.zeros((T, E), xt.dtype).at[jnp.arange(T)[:, None], idx].add(w)
            h = jax.nn.silu(jnp.einsum('td,ehd->teh', xt, W1)) * jnp.einsum('td,ehd->teh', xt, W3)
            out = jnp.einsum('teh,edh->ted', h, W2)
            y = jnp.einsum('te,ted->td', cw, out)
            return y.reshape(B, S, D)
        return _moe_forward(x, Wg, W1, W2, W3)
    x = L0_attn_x
    xn = _layernorm(x, axis=-1)
    x = x + _L0_attn_ref(xn, L0_attn_W_Q, L0_attn_W_K, L0_attn_W_V, L0_attn_W_O) + _L0_ffn_ref(xn, L0_ffn_Wg, L0_ffn_W1, L0_ffn_W2, L0_ffn_W3)
    return x

_drawn_inputs = setup_inputs


def setup_inputs(seed=0):
    import zlib

    import numpy as np

    out = dict(_drawn_inputs(seed))
    spreads = {}
    factors = {'L0_ffn_Wg': 8.0,
     'L0_ffn_W1': 8.0,
     'L0_ffn_W2': 8.0,
     'L0_ffn_W3': 8.0,
     'L0_attn_W_Q': 3.713,
     'L0_attn_W_K': 3.636,
     'L0_attn_W_V': 3.174,
     'L0_attn_W_O': 3.156}
    for name, (base, spread) in spreads.items():
        noise = np.random.default_rng([zlib.crc32(name.encode()), seed]).standard_normal(out[name].shape)
        drawn = base * np.exp(spread * noise) if base else spread * noise
        out[name] = jnp.asarray(drawn.astype(out[name].dtype))
    for name, factor in factors.items():
        out[name] = (out[name] * factor).astype(out[name].dtype)
    return out
```

```python
from contextlib import ExitStack

import concourse.bass as bass
from concourse import mybir

F32 = mybir.dt.float32
BF16 = mybir.dt.bfloat16
ALU = mybir.AluOpType
ACT = mybir.ActivationFunctionType
AX = mybir.AxisListType

P = 128
B, L, D = 8, 512, 128
H, HD = 16, 8
NT = L // P
TILES = B * NT
E, HID, TOPK = 8, 352, 2
EPS = 1e-5
G = 4
GROUPS = H // G
STEPS = GROUPS * NT
PAIRS = H // 2
TERMS = 6
ROWS = 2 * TERMS * HD
MROWS = 2 * 3
Q_TERMS = [0, 1, 2, 0, 1, 0]
K_TERMS = [0, 0, 0, 1, 1, 2]
CH = [(0, 128), (128, 128), (256, 96)]

USES = [
    (1, "A", "maxT", 1), (2, "A", "ctxT", -1), (3, "A", "ctxnT", -1), (4, "A", "out", -1),
    (5, "A", "maxT", 2), (6, "A", "ctxT", 0), (7, "A", "xnT", 2),
    (8, "A", "v0", 2), (8, "B", "v1", 2), (9, "A", "maxT", 3), (10, "A", "ctxT", 1), (10, "B", "q", 2),
    (11, "A", "qrot", 2), (11, "B", "k", 2), (12, "A", "krot", 2), (13, "A", "maxT", 4), (14, "A", "ctxT", 2),
]
PREP = ("xnT", "v0", "v1", "q", "qrot", "k", "krot")


def active(b, use):
    _, _, kind, rel = use
    if kind in ("maxT", "ctxT"):
        return 0 <= GROUPS * b + rel < GROUPS * B
    return 0 <= b + rel < B


ORDER = {}
for _b in range(-2, B + 1):
    for _u in USES:
        if active(_b, _u):
            ORDER[(_b, _u[2], _u[3])] = len(ORDER)


def at(base, slope, d):
    return base + slope * d if not isinstance(d, int) else base + slope * d


def block_kernel(nc, x, w_q, w_k, w_v, w_o, w_g, w1, w2, w3, cos_t, sin_t, out):
    with ExitStack() as ctx:
        def sb(name, shape, dt=F32):
            return ctx.enter_context(nc.sbuf_tensor(name, shape, dt))

        def sem(name):
            return ctx.enter_context(nc.semaphore(name))

        ps = ctx.enter_context(nc.psum_tensor("ps", [P, 8, 512], F32))
        ps_s = ps[:, 0:2, :]
        ps_m = ps[:, 2:6, :]
        ps_ctx = ps[:, 6, :]
        ps_misc = ps[:, 7, :]

        x_sb = sb("x_sb", [P, TILES, D])
        xnT_all = sb("xnT_all", [P, TILES * P])
        logits = sb("logits", [P, TILES, E])
        wqT, wkT = sb("wqT", [P, D]), sb("wkT", [P, D])
        wqr, wkr = sb("wqr", [P, D]), sb("wkr", [P, D])
        wvg = sb("wvg", [P, D + E])
        woT = sb("woT", [P, D])
        cos_sb, sin_sb = sb("cos_sb", [P, L]), sb("sin_sb", [P, L])
        ident = sb("ident", [P, P])
        ident_bf = sb("ident_bf", [P, P], BF16)
        w1_sb = sb("w1_sb", [P, E, HID])
        w3_sb = sb("w3_sb", [P, E, HID])
        w2_sb = sb("w2_sb", [P, E, 3, D])
        stats = sb("stats", [P, TILES, 6])
        mv = sb("mv", [P, TILES, 2])
        var, root, rstd = sb("var", [P, TILES]), sb("root", [P, TILES]), sb("rstd", [P, TILES])
        xn = sb("xn", [P, NT, D])
        xnT = sb("xnT", [P, L])
        v_stage = sb("v_stage", [P, NT, D])
        v_st = [sb(f"v_st{i}", [P, NT, H, 32]) for i in range(2)]
        rope_a, rope_b = sb("rope_a", [P, 2, L]), sb("rope_b", [P, 2, L])
        rest = sb("rest", [P, 2, L])
        parts = sb("parts", [P, 2, 3, L], BF16)
        q_st = [sb(f"q_st{i}", [P, PAIRS, L], BF16) for i in range(2)]
        k_st = [sb(f"k_st{i}", [P, H, L], BF16) for i in range(2)]
        negm = sb("negm", [P, 2, NT, G])
        mrest = sb("mrest", [P, NT, G])
        msplit = sb("msplit", [P, NT, G, 3], BF16)
        mrow = sb("mrow", [G * 3, L], BF16)
        probs = sb("probs", [P, 8, L])
        ctx_sb = sb("ctx_sb", [P, L])
        ctx_r = sb("ctx_r", [P, NT, G])
        ctxn = sb("ctxn", [P, NT, D])
        ctxnT = sb("ctxnT", [P, L])
        r_e = sb("r_e", [P, TILES, E])
        r_s = sb("r_s", [P, TILES, E])
        r_rank = sb("r_rank", [P, TILES, E])
        r_cmp = sb("r_cmp", [P, TILES, E])
        r_one = sb("r_one", [P, TILES])
        cw = sb("cw", [P, TILES, E])
        xcur = [sb(f"xcur{i}", [P, P]) for i in range(2)]
        gate = [sb(f"gate{i}", [P, HID]) for i in range(2)]
        hid = [sb(f"hid{i}", [P, HID]) for i in range(2)]
        hidT = [sb(f"hidT{i}", [P, 3, P]) for i in range(2)]

        q_dram = nc.dram_tensor("q_terms", (2, 2, TERMS, HD * H, L), BF16).ap()

        x_first, x_rest, w_loaded, ffn_w_loaded = sem("x_first"), sem("x_rest"), sem("w_loaded"), sem("ffn_w_loaded")
        consts = sem("consts")
        rot_made = sem("rot_made")
        scores_made, probs_made = sem("scores_made"), sem("probs_made")
        pv_done, ctx_copied = sem("pv_done"), sem("ctx_copied")
        max_scores, max_found = sem("max_scores"), sem("max_found")
        max_split, max_rows = sem("max_split"), sem("max_rows")
        misc_filled, misc_emptied = sem("misc_filled"), sem("misc_emptied")
        xn_made, v_placed, parts_made = sem("xn_made"), sem("v_placed"), sem("parts_made")
        terms_written, stacks_loaded = sem("terms_written"), sem("stacks_loaded")
        xnT_kept = sem("xnT_kept")
        dve_seq, pool_seq, stat_seq = sem("dve_seq"), sem("pool_seq"), sem("stat_seq")
        var_made, root_made = sem("var_made"), sem("root_made")
        r_exp, r_shift, cw_made = sem("r_exp"), sem("r_shift"), sem("cw_made")
        xcur_made, ab_made, gate_made, hid_made = sem("xcur_made"), sem("ab_made"), sem("gate_made"), sem("hid_made")
        hT_made, hidT_made, y_made, y_added = sem("hT_made"), sem("hidT_made"), sem("y_made"), sem("y_added")
        stored = sem("stored")

        block = ctx.enter_context(nc.Block())
        x_dram = x.rearrange("b (t p) d -> b p t d", p=P)
        out_dram = out.rearrange("b (t p) d -> b p t d", p=P)

        def wait(eng, semaphore, value):
            if not isinstance(value, int):
                value = eng.to_reg(value)
                eng.wait_ge(x_first, 16)
            eng.wait_ge(semaphore, value)

        def use_no(b, kind, rel, d):
            return at(ORDER[(b, kind, rel)], len(USES), d)

        def uses(b, s, slot):
            return [u for u in USES if u[0] == s and u[1] == slot and active(b, u)]

        def pipeline(eng, step):
            for b in (-2, -1):
                for s in range(STEPS):
                    step(b, s, 0)
            for s in range(5):
                step(0, s, 0)
            with eng.Fori(0, (B - 2) // 2) as it:
                for u in (0, 1):
                    for s in range(5, STEPS):
                        step(u, s, it * 2)
                    for s in range(5):
                        step(u + 1, s, it * 2)
            for s in range(5, STEPS):
                step(B - 2, s, 0)
            for s in range(STEPS):
                step(B - 1, s, 0)
            for s in range(5):
                step(B, s, 0)

        @block.sync
        def _(sp):
            sp.dma_start(x_sb[:, 0:NT, :], x_dram[0]).then_inc(x_first, 16)
            for src, dst in ((w_q, wqT[:]), (w_k, wkT[:]), (w_v, wvg[:, 0:D]), (w_g, wvg[:, D:D + E]), (w_o, woT[:]),
                             (cos_t, cos_sb[:]), (sin_t, sin_sb[:])):
                sp.dma_start(dst, src).then_inc(w_loaded, 16)
            for b in range(1, B):
                sp.dma_start(x_sb[:, NT * b:NT * (b + 1), :], x_dram[b]).then_inc(x_rest, 16)
            sp.dma_start(w1_sb[:], w1).then_inc(ffn_w_loaded, 16)
            sp.dma_start(w3_sb[:], w3).then_inc(ffn_w_loaded, 16)
            for c, (h0, n) in enumerate(CH):
                sp.dma_start(w2_sb[0:n, :, c, :], w2[h0:h0 + n]).then_inc(ffn_w_loaded, 16)

            def step(b, s, d):
                par = (b + 1) % 2
                if s == 0 and 0 <= b + 1 < B:
                    wait(sp, parts_made, at(b + 2, 1, d))
                    if b + 1 >= 1:
                        wait(sp, stacks_loaded, at(4 * 16 * (b + 1), 64, d))
                    for qk, terms in enumerate((Q_TERMS, K_TERMS)):
                        for t, part in enumerate(terms):
                            sp.dma_start(q_dram[par, qk, t], parts[:, qk, part, :]).then_inc(terms_written, 16)
                if s == 2 and 0 <= b + 1 < B:
                    wait(sp, terms_written, at(2 * TERMS * 16 * (b + 2), 2 * TERMS * 16, d))
                    if b + 1 >= 2:
                        wait(sp, scores_made, at(4 * STEPS * b, 4 * STEPS, d))
                    for qk in (0, 1):
                        for hh in (0, 1):
                            r0 = hh * TERMS * HD
                            src = q_dram[par, qk].rearrange("t (d p two) l -> two (t d) p l", two=2, d=HD)[hh]
                            dst = q_st[par][r0:r0 + TERMS * HD, :, :] if qk == 0 else \
                                k_st[par][r0:r0 + TERMS * HD, hh:H:2, :]
                            sp.dma_start(dst, src).then_inc(stacks_loaded, 16)
                for u in USES:
                    if u[0] == s and u[2] == "maxT" and active(b, u):
                        grp, n = GROUPS * b + u[3], use_no(b, "maxT", u[3], d)
                        wait(sp, misc_emptied, n + 1)
                        pb = (b + u[3] // GROUPS) % 2
                        for pr in range(G // 2):
                            sp.dma_start(q_st[pb][ROWS:ROWS + MROWS, 2 * (u[3] % GROUPS) + pr, :],
                                         mrow[MROWS * pr:MROWS * (pr + 1), :]).then_inc(max_rows, 16)

            pipeline(sp, step)
            for b in range(B):
                wait(sp, y_added, E * NT * (b + 1))
                sp.dma_start(out_dram[b], x_sb[:, NT * b:NT * (b + 1), :]).then_inc(stored, 16)
            wait(sp, stored, 16 * B)

        @block.tensor
        def _(pe):
            pe.wait_ge(w_loaded, 7 * 16)
            pe.wait_ge(consts, 3)
            pe.wait_ge(rot_made, 1)

            def shared(b, u, d):
                kind, rel = u[2], u[3]
                n = use_no(b, kind, rel, d)
                if ORDER[(b, kind, rel)] > 0:
                    pe.wait_ge(misc_emptied, n)
                if kind == "maxT":
                    pe.wait_ge(max_split, at(GROUPS * b + rel + 1, GROUPS, d))
                    dst = ps_misc.bitcast(BF16)
                    for qb in range(NT):
                        last = nc.tensor.transpose(dst[0:3 * G, qb * P:(qb + 1) * P],
                                                   msplit[:, qb].rearrange("p g t -> p (g t)"), ident_bf[:])
                elif kind == "ctxT":
                    pe.wait_ge(ctx_copied, at(GROUPS * b + rel + 1, GROUPS, d))
                    for qb in range(NT):
                        last = nc.tensor.transpose(ps_misc[:, qb * P:(qb + 1) * P],
                                                   ctx_sb[:, qb * P:(qb + 1) * P], ident[:])
                elif kind == "ctxnT":
                    for qb in range(NT):
                        last = nc.tensor.transpose(ps_misc[:, qb * P:(qb + 1) * P], ctxn[:, qb, :], ident[:])
                elif kind == "out":
                    for qb in range(NT):
                        last = nc.tensor.matmul(ps_misc[:, qb * P:(qb + 1) * P], ctxnT[:, qb * P:(qb + 1) * P],
                                                woT[:], start=True, stop=True)
                elif kind == "xnT":
                    pe.wait_ge(xn_made, at(b + rel + 1, 1, d))
                    for t in range(NT):
                        last = nc.tensor.transpose(ps_misc[:, t * P:(t + 1) * P], xn[:, t, :], ident[:])
                elif kind in ("v0", "v1"):
                    t0 = 2 * int(kind[1])
                    for t in (0, 1):
                        last = nc.tensor.matmul(ps_misc[:, t * (D + E):(t + 1) * (D + E)],
                                                xnT[:, (t0 + t) * P:(t0 + t + 1) * P], wvg[:], start=True, stop=True)
                else:
                    w = {"q": wqT, "qrot": wqr, "k": wkT, "krot": wkr}[kind]
                    last = nc.tensor.matmul(ps_misc[:], w[:], xnT[:], start=True, stop=True)
                last.then_inc(misc_filled, 1)

            def step(b, s, d):
                g, kb = s // NT, s % NT
                par, live = b % 2, 0 <= b < B
                grp = GROUPS * b + g + 2
                find = 0 <= grp < GROUPS * B
                mb, mg = (b + (g + 2) // GROUPS) % 2, (g + 2) % GROUPS
                if live and kb == 0:
                    pe.wait_ge(max_rows, at(32 * (GROUPS * b + g + 1), 32 * GROUPS, d))
                if find and s % (2 * NT) == 0 and mg == 0:
                    pe.wait_ge(stacks_loaded, at(64 * (grp // GROUPS + 1), 64, d))
                for half in (0, 1):
                    if live:
                        for j in (2 * half, 2 * half + 1):
                            n = 4 * (STEPS * b + s) + j
                            if n >= 2:
                                pe.wait_ge(probs_made, at(n - 1, 4 * STEPS, d))
                            h = G * g + j
                            nc.tensor.matmul(ps_s[:, j % 2, :],
                                             k_st[par][0:ROWS + MROWS, h, kb * P:(kb + 1) * P],
                                             q_st[par][0:ROWS + MROWS, h // 2, :],
                                             start=True, stop=True).then_inc(scores_made, 1)
                    if find:
                        h = G * mg + kb
                        m = 2 * (NT * grp + kb) + half
                        if m >= 2:
                            pe.wait_ge(max_found, at(m - 1, 2 * STEPS, d))
                        for i in (0, 1):
                            qb = 2 * half + i
                            last = nc.tensor.matmul(ps_m[:, 2 * half + i, :],
                                                    q_st[mb][0:ROWS, h // 2, qb * P:(qb + 1) * P],
                                                    k_st[mb][0:ROWS, h, :], start=True, stop=True)
                        last.then_inc(max_scores, 1)
                for u in uses(b, s, "A"):
                    shared(b, u, d)
                n = STEPS * b + s - 1
                if 0 <= n < STEPS * B:
                    pb, ps_ = (b if s else b - 1) % 2, (s - 1) % STEPS
                    pg, pk = ps_ // NT, ps_ % NT
                    pe.wait_ge(probs_made, at(4 * (n + 1), 4 * STEPS, d))
                    if pk == 0 and n >= NT:
                        pe.wait_ge(ctx_copied, at(n // NT, GROUPS, d))
                    if pk == 0 and pg == 0:
                        pe.wait_ge(v_placed, at(n // STEPS + 1, 1, d))
                    for j in range(G):
                        last = nc.tensor.matmul(ps_ctx[32 * j:32 * j + 32, :], v_st[pb][:, pk, G * pg + j, :],
                                                probs[:, 4 * (ps_ % 2) + j, :], start=(pk == 0), stop=(pk == NT - 1))
                    last.then_inc(pv_done, 1)
                for u in uses(b, s, "B"):
                    shared(b, u, d)

            pipeline(pe, step)

            pe.wait_ge(ffn_w_loaded, 5 * 16)
            pe.wait_ge(misc_emptied, len(ORDER))
            pe.wait_ge(probs_made, 4 * STEPS * B)
            pe.wait_ge(max_found, 2 * STEPS * B)
            pe.wait_ge(ctx_copied, GROUPS * B)

            def up(n, e, u, d):
                if e == 0:
                    pe.wait_ge(xcur_made, n // E + 1 if isinstance(d, int) else d + (u + 1))
                if not (isinstance(d, int) and n < 2):
                    pe.wait_ge(hid_made, (n - 1) if isinstance(d, int) else E * d + (E * u + e - 1))
                for w, k in ((w1_sb, 0), (w3_sb, 1)):
                    last = nc.tensor.matmul(ps[:, 2 * (e % 2) + k, 0:HID], xcur[u][:], w[:, e, :],
                                            start=True, stop=True)
                last.then_inc(ab_made, 1)

            def down(n):
                c, d = n
                e = c % E
                v = c if d is None else E * d + c
                pe.wait_ge(hid_made, v + 1)
                if not (d is None and c < 2):
                    pe.wait_ge(hidT_made, v - 1)
                for i, (h0, m) in enumerate(CH):
                    last = nc.tensor.transpose(ps[0:m, 4 + e % 2, i * P:(i + 1) * P], hid[e % 2][:, h0:h0 + m],
                                               ident[:])
                last.then_inc(hT_made, 1)

            def down2(n):
                c, d = n
                e = c % E
                v = c if d is None else E * d + c
                pe.wait_ge(hidT_made, v + 1)
                if not (d is None and c < 2):
                    pe.wait_ge(y_added, v - 1)
                for i, (h0, m) in enumerate(CH):
                    last = nc.tensor.matmul(ps[:, 6 + e % 2, 0:D], hidT[e % 2][0:m, i, :], w2_sb[0:m, e, i, :],
                                            start=(i == 0), stop=(i == 2))
                last.then_inc(y_made, 1)

            def tile(u, d, first):
                for e in range(E):
                    c = E * u + e
                    n = (c, None) if d is None else (c, d)
                    up(c, e, u % 2, 0 if d is None else d)
                    if not (first and c < 1):
                        down((c - 1, d))
                    if not (first and c < 2):
                        down2((c - 2, d))

            tile(0, None, True)
            tile(1, None, False)
            with pe.Fori(1, TILES // 2) as it:
                tile(0, it * 2, False)
                tile(1, it * 2, False)
            down((E * TILES - 1, None))
            down2((E * TILES - 2, None))
            down2((E * TILES - 1, None))

        @block.scalar
        def _(act):
            def shared(b, u, d):
                kind, rel = u[2], u[3]
                if kind not in ("maxT", "ctxnT", "xnT", "v0", "v1"):
                    return
                n = use_no(b, kind, rel, d)
                act.wait_ge(misc_filled, n + 1)
                if kind == "maxT":
                    if GROUPS * b + rel >= 1:
                        act.wait_ge(max_rows, at(32 * (GROUPS * b + rel), 32 * GROUPS, d))
                    nc.scalar.copy(mrow[:], ps_misc.bitcast(BF16)[0:3 * G, 0:L]).then_inc(misc_emptied, 1)
                elif kind == "ctxnT":
                    nc.scalar.copy(ctxnT[:], ps_misc[:]).then_inc(misc_emptied, 1)
                elif kind == "xnT":
                    if b + rel >= 1:
                        act.wait_ge(xnT_kept, at(b + rel, 1, d))
                    nc.scalar.copy(xnT[:], ps_misc[:]).then_inc(misc_emptied, 1)
                else:
                    t0 = 2 * int(kind[1])
                    if kind == "v0" and b + rel >= 1:
                        act.wait_ge(v_placed, at(b + rel, 1, d))
                    both = ps_misc[:, 0:2 * (D + E)].rearrange("p (t n) -> p t n", t=2)
                    nc.scalar.copy(v_stage[:, t0:t0 + 2, :], both[:, :, 0:D])
                    nc.scalar.copy(logits[:, bass.ds(at(NT * (b + rel) + t0, NT, d), 2), :],
                                   both[:, :, D:D + E]).then_inc(misc_emptied, 1)

            def step(b, s, d):
                live = 0 <= b < B
                if b < 0 and s == 0:
                    t0, t1 = (0, NT) if b == -2 else (NT, TILES)
                    act.wait_ge(var_made, b + 3)
                    nc.scalar.activation(root[:, t0:t1], var[:, t0:t1], ACT.Sqrt).then_inc(root_made, 1)

                def exps(j0):
                    for j in (j0, j0 + 1):
                        n = 4 * (STEPS * b + s) + j
                        if j % 4 == 0 and n >= 8:
                            act.wait_ge(pv_done, at(n // 4 - 1, STEPS, d))
                        act.wait_ge(scores_made, at(n + 1, 4 * STEPS, d))
                        nc.scalar.activation(probs[:, n % 8, :], ps_s[:, j % 2, :], ACT.Exp,
                                             scale=float(HD) ** -0.5).then_inc(probs_made, 1)

                if live:
                    exps(0)
                pb, psn = (b, s - 1) if s else (b - 1, STEPS - 1)
                for u in USES:
                    if (u[0], u[1]) == (psn, "B") and s and active(b, u):
                        shared(b, u, d)
                n = STEPS * b + s - 1
                if n >= NT and n % NT == 0 and n // NT <= GROUPS * B:
                    grp = n // NT - 1
                    act.wait_ge(pv_done, at(n, STEPS, d))
                    if grp >= 1:
                        key = (grp - 1) - GROUPS * b
                        act.wait_ge(misc_filled, ctx_use(grp - 1, b, d) + 1)
                    nc.scalar.copy(ctx_sb[:], ps_ctx[:]).then_inc(ctx_copied, 1)
                if live:
                    exps(2)
                for u in uses(b, s, "A"):
                    shared(b, u, d)

            def ctx_use(grp, b, d):
                for (bb, kind, rel), n in ORDER.items():
                    if kind == "ctxT" and GROUPS * bb + rel == grp:
                        return at(n, len(USES), d)

            pipeline(act, step)

            act.wait_ge(r_shift, 1)
            nc.scalar.activation(r_e[:], r_s[:], ACT.Exp).then_inc(r_exp, 1)

            def pair(c, d):
                e = c % E
                v = c if d is None else E * d + c
                act.wait_ge(ab_made, v + 1)
                if not (d is None and c < 2):
                    act.wait_ge(hid_made, v - 1)
                nc.scalar.activation(gate[e % 2][:], ps[:, 2 * (e % 2), 0:HID], ACT.Silu).then_inc(gate_made, 1)
                if d is None and c < 1:
                    return
                back(c - 1, d)

            def back(c, d):
                v = c if d is None else E * d + c
                e = c % E
                act.wait_ge(hT_made, v + 1)
                if not (d is None and c < 2):
                    act.wait_ge(y_made, v - 1)
                nc.scalar.copy(hidT[e % 2][:, 0:2, :], ps[:, 4 + e % 2, 0:2 * P].rearrange("p (c n) -> p c n", c=2))
                nc.scalar.copy(hidT[e % 2][0:96, 2, :], ps[0:96, 4 + e % 2, 2 * P:3 * P]).then_inc(hidT_made, 1)

            for c in range(2 * E):
                pair(c, None)
            with act.Fori(1, TILES // 2) as it:
                for c in range(2 * E):
                    pair(c, it * 2)
            back(E * TILES - 1, None)

        @block.vector
        def _(dve):
            count = [0]

            def link(ins, per=None):
                ins.then_inc(dve_seq, 1)
                return ins

            for i in (0, 1):
                nc.vector.memset(v_st[i][:], 0.0).then_inc(consts, 1)
            dve.wait_ge(w_loaded, 7 * 16)
            for src, dst in ((wqT, wqr), (wkT, wkr)):
                s2, d2 = (a[:].rearrange("p (n two h) -> p n two h", two=2, h=H) for a in (src, dst))
                nc.vector.tensor_scalar(d2[:, :, 0, :], s2[:, :, 1, :], -1.0, None, ALU.mult)
                last = nc.vector.tensor_copy(d2[:, :, 1, :], s2[:, :, 0, :])
            last.then_inc(rot_made, 1)

            seq_at, tot = {}, 2 * 4
            for bb in range(-2, B + 1):
                for u in USES:
                    if u[2] == "ctxT" and active(bb, u):
                        seq_at[("ctx", bb, u[3])] = tot
                        tot += 1
            PER = GROUPS

            def statistics(no, t0, t1):
                base = 4 * no
                for t in range(t0, t1):
                    last = nc.vector.bn_stats(stats[:, t, :], x_sb[:, t, :])
                link(last)
                dve.wait_ge(dve_seq, base + 1)
                for t in range(t0, t1):
                    last = nc.vector.bn_aggr(mv[:, t, :], stats[:, t, :])
                link(last)
                dve.wait_ge(dve_seq, base + 2)
                nc.vector.tensor_scalar(var[:, t0:t1], mv[:, t0:t1, 1], EPS, None, ALU.add).then_inc(var_made, 1)
                dve.wait_ge(root_made, no + 1)
                nc.vector.reciprocal(rstd[:, t0:t1], root[:, t0:t1]).then_inc(stat_seq, 1)
                dve.wait_ge(stat_seq, 3 * no + 1)
                link(nc.vector.tensor_tensor(rstd[:, t0:t1], var[:, t0:t1], rstd[:, t0:t1], ALU.mult))
                dve.wait_ge(dve_seq, base + 3)
                link(nc.vector.tensor_tensor(root[:, t0:t1], rstd[:, t0:t1], root[:, t0:t1], ALU.add))
                dve.wait_ge(dve_seq, base + 4)
                nc.vector.tensor_scalar(root[:, t0:t1], root[:, t0:t1], 0.5, None, ALU.mult).then_inc(stat_seq, 1)
                dve.wait_ge(stat_seq, 3 * no + 2)
                nc.vector.reciprocal(rstd[:, t0:t1], root[:, t0:t1]).then_inc(stat_seq, 1)
                dve.wait_ge(stat_seq, 3 * no + 3)

            def layer_norm(b, d):
                if b == -2:
                    dve.wait_ge(x_first, 16)
                    statistics(0, 0, NT)
                if b + 2 >= 1:
                    dve.wait_ge(misc_filled, use_no(b - 1, "xnT", 2, d) + 1)
                for t in range(NT):
                    nt = bass.ds(at(NT * (b + 2) + t, NT, d), 1)
                    last = nc.vector.tensor_scalar(xn[:, t, :], x_sb[:, nt, :].rearrange("p a n -> p (a n)"),
                                                   mv[:, nt, 0], rstd[:, nt], ALU.subtract, ALU.mult)
                last.then_inc(xn_made, 1)

            def shared(b, u, d):
                kind, rel = u[2], u[3]
                if kind in ("maxT", "ctxnT", "xnT", "v0", "v1"):
                    return
                n = use_no(b, kind, rel, d)
                dve.wait_ge(misc_filled, n + 1)
                if kind == "ctxT":
                    g = (GROUPS + rel) % GROUPS
                    t4 = ps_misc.rearrange("p (q j c) -> p q j c", q=NT, j=G)
                    link(nc.vector.reciprocal(ctx_r[:], t4[:, :, :, HD]))
                    dve.wait_ge(dve_seq, at(seq_at[("ctx", b, rel)] + 1, PER, d))
                    nc.vector.tensor_tensor(
                        ctxn[:, :, g * G * HD:(g + 1) * G * HD].rearrange("p q (j c) -> p q j c", j=G),
                        t4[:, :, :, 0:HD], ctx_r[:].rearrange("p q (j one) -> p q j one", one=1).to_broadcast(
                            [P, NT, G, HD]), ALU.mult).then_inc(misc_emptied, 1)
                elif kind == "out":
                    sl = x_sb[:, bass.ds(at(NT * (b + rel), NT, d), NT), :]
                    nc.vector.tensor_tensor(sl, ps_misc.rearrange("p (t n) -> p t n", t=NT), sl,
                                            ALU.add).then_inc(misc_emptied, 1)
                else:
                    if kind == "q" and b + rel >= 1:
                        dve.wait_ge(parts_made, at(b + rel, 1, d))
                    dst = (rope_a if kind in "qk" else rope_b)[:, 0 if kind[0] == "q" else 1, :]
                    nc.vector.tensor_tensor(dst, ps_misc[:], (cos_sb if kind in "qk" else sin_sb)[:],
                                            ALU.mult).then_inc(misc_emptied, 1)

            def step(b, s, d):
                g, kb = s // NT, s % NT
                grp = GROUPS * b + g + 2
                if 0 <= grp < GROUPS * B:
                    if kb == 0 and grp >= 2:
                        dve.wait_ge(max_split, at(grp - 1, GROUPS, d))
                    for half in (0, 1):
                        m = 2 * (NT * grp + kb) + half
                        dve.wait_ge(max_scores, at(m + 1, 2 * STEPS, d))
                        nc.vector.tensor_reduce(negm[:, g % 2, 2 * half:2 * half + 2, kb],
                                                ps_m[:, 2 * half:2 * half + 2, :], axis=AX.X, op=ALU.max,
                                                negate=True).then_inc(max_found, 1)
                if s == 0 and b == -1:
                    dve.wait_ge(x_rest, 16 * (B - 1))
                    statistics(1, NT, TILES)
                if s == 5 and 0 <= b + 2 < B:
                    layer_norm(b, d)
                for slot in "AB":
                    for u in uses(b, s, slot):
                        shared(b, u, d)

            pipeline(dve, step)

            chain = [tot]

            def then(ins):
                chain[0] += 1
                ins.then_inc(dve_seq, 1)
                dve.wait_ge(dve_seq, chain[0])

            def over(a, n=E):
                return a.rearrange("p (t one) -> p t one", one=1).to_broadcast([P, TILES, n])

            dve.wait_ge(misc_emptied, len(ORDER))
            then(nc.vector.tensor_reduce(r_one[:], logits[:], axis=AX.X, op=ALU.max))
            nc.vector.tensor_tensor(r_s[:], logits[:], over(r_one[:]), ALU.subtract).then_inc(r_shift, 1)
            dve.wait_ge(r_exp, 1)
            then(nc.vector.tensor_reduce(r_one[:], r_e[:], axis=AX.X, op=ALU.add))
            then(nc.vector.reciprocal(r_one[:], r_one[:]))
            then(nc.vector.tensor_tensor(r_s[:], r_e[:], over(r_one[:]), ALU.mult))
            then(nc.vector.memset(r_rank[:], 0.0))
            for j in range(E):
                col = r_s[:, :, j:j + 1]
                if j + 1 < E:
                    nc.vector.tensor_tensor(r_cmp[:, :, j + 1:E], col.to_broadcast([P, TILES, E - j - 1]),
                                            r_s[:, :, j + 1:E], ALU.is_ge)
                then(nc.vector.tensor_tensor(r_cmp[:, :, 0:j + 1], col.to_broadcast([P, TILES, j + 1]),
                                             r_s[:, :, 0:j + 1], ALU.is_gt))
                then(nc.vector.tensor_tensor(r_rank[:], r_rank[:], r_cmp[:], ALU.add))
            then(nc.vector.tensor_scalar(r_cmp[:], r_rank[:], float(TOPK), None, ALU.is_lt))
            then(nc.vector.tensor_tensor(r_cmp[:], r_cmp[:], r_s[:], ALU.mult))
            then(nc.vector.tensor_reduce(r_one[:], r_cmp[:], axis=AX.X, op=ALU.add))
            then(nc.vector.tensor_scalar(r_one[:], r_one[:], 1e-20, None, ALU.add))
            then(nc.vector.reciprocal(r_one[:], r_one[:]))
            then(nc.vector.tensor_tensor(cw[:], r_cmp[:], over(r_one[:]), ALU.mult))

            def pair(c, d, t_reg, t_off):
                e = c % E
                v = c if d is None else E * d + c
                dve.wait_ge(gate_made, v + 1)
                if not (d is None and c < 2):
                    dve.wait_ge(hT_made, v - 1)
                nc.vector.tensor_tensor(hid[e % 2][:], gate[e % 2][:], ps[:, 2 * (e % 2) + 1, 0:HID],
                                        ALU.mult).then_inc(hid_made, 1)
                if d is None and c < 2:
                    return
                add(c - 2, d)

            def add(c, d):
                e = c % E
                v = c if d is None else E * d + c
                dve.wait_ge(y_made, v + 1)
                if not (d is None and c == 0):
                    dve.wait_ge(y_added, v)
                if d is None:
                    t = c // E
                    xs, w = x_sb[:, t, :], cw[:, t, e:e + 1]
                else:
                    t = d + c // E if c >= 0 else d - 1
                    xs = x_sb[:, bass.ds(t, 1), :].rearrange("p a n -> p (a n)")
                    w = cw[:, bass.ds(t, 1), e:e + 1].rearrange("p a n -> p (a n)")
                nc.vector.scalar_tensor_tensor(xs, ps[:, 6 + e % 2, 0:D], w, xs,
                                               op0=ALU.mult, op1=ALU.add).then_inc(y_added, 1)

            for c in range(2 * E):
                pair(c, None, None, None)
            with dve.Fori(1, TILES // 2) as it:
                for c in range(2 * E):
                    pair(c, it * 2, None, None)
            add(E * TILES - 2, None)
            add(E * TILES - 1, None)

        @block.gpsimd
        def _(pool):
            made = [0]

            def then(ins):
                made[0] += 1
                ins.then_inc(pool_seq, 1)
                pool.wait_ge(pool_seq, made[0])

            then(nc.gpsimd.memset(ident[:], 0.0))
            then(nc.gpsimd.affine_select(out=ident[:], in_=ident[:], compare_op=ALU.not_equal, fill=1.0, base=0,
                                         pattern=[[-1, P]], channel_multiplier=1))
            then(nc.gpsimd.tensor_copy(ident_bf[:], ident[:]))
            for i in (0, 1):
                then(nc.gpsimd.memset(k_st[i][:], 0.0))
                for hh, base, sign in ((0, 2, -1), (1, -3, 1)):
                    v = k_st[i][ROWS:P, hh:H:2, :]
                    then(nc.gpsimd.memset(v, 1.0))
                    then(nc.gpsimd.affine_select(out=v, in_=v, compare_op=ALU.is_ge, fill=0.0, base=base,
                                                 pattern=[[0, PAIRS], [0, L]], channel_multiplier=sign))
            pool.wait_ge(consts, 2)
            for i in (0, 1):
                last = nc.gpsimd.memset(v_st[i][:, :, :, HD:HD + 1], 1.0)
            last.then_inc(consts, 1)

            M_LINKS, S_LINKS = 3, 5
            seq_at, tot = {}, made[0]
            for bb in range(-2, B + 1):
                for ss in range(STEPS):
                    if ss % NT == 0 and 0 <= GROUPS * bb + ss // NT + 1 < GROUPS * B:
                        seq_at[("m", bb, ss)] = tot
                        tot += M_LINKS
                    if ss == 12 and 0 <= bb + 2 < B:
                        seq_at[("s", bb)] = tot
                        tot += 2 * S_LINKS - 1
            PER = GROUPS * M_LINKS + 2 * S_LINKS - 1

            def link(ins, base, i, d):
                ins.then_inc(pool_seq, 1)
                wait(pool, pool_seq, at(base + i, PER, d))

            def step(b, s, d):
                g, kb = s // NT, s % NT
                grp = GROUPS * b + g + 1
                if kb == 0 and 0 <= grp < GROUPS * B:
                    base = seq_at[("m", b, s)]
                    wait(pool, max_found, at(2 * NT * (grp + 1), 2 * STEPS, d))
                    if grp >= 1:
                        bb, rel = (b, g) if g else (b - 1, GROUPS)
                        wait(pool, misc_filled, use_no(bb, "maxT", rel, d) + 1)
                    src = negm[:, (g + 1) % 2]
                    link(nc.gpsimd.tensor_copy(msplit[:, :, :, 0], src), base, 1, d)
                    link(nc.gpsimd.tensor_tensor(mrest[:], src, msplit[:, :, :, 0], ALU.subtract), base, 2, d)
                    link(nc.gpsimd.tensor_copy(msplit[:, :, :, 1], mrest[:]), base, 3, d)
                    nc.gpsimd.tensor_tensor(msplit[:, :, :, 2], mrest[:], msplit[:, :, :, 1],
                                            ALU.subtract).then_inc(max_split, 1)
                if s == 1 and 0 <= b + 1 < B:
                    wait(pool, misc_emptied, use_no(b - 1, "v1", 2, d) + 1)
                    if b >= 1:
                        wait(pool, pv_done, at(STEPS * b, STEPS, d))
                    last = None
                    for t in range(NT):
                        last = nc.gpsimd.tensor_copy(v_st[(b + 1) % 2][:, t, :, 0:HD],
                                                     v_stage[:, t, :].rearrange("p (h c) -> p h c", h=H))
                    last.then_inc(v_placed, 1)
                if s == 8 and 0 <= b + 2 < B:
                    wait(pool, misc_emptied, use_no(b, "xnT", 2, d) + 1)
                    nc.gpsimd.tensor_copy(xnT_all[:, bass.ds(at(L * (b + 2), L, d), L)], xnT[:]).then_inc(xnT_kept, 1)
                if s == 12 and 0 <= b + 2 < B:
                    base = seq_at[("s", b)]
                    if b + 2 >= 1:
                        wait(pool, terms_written, at(2 * TERMS * 16 * (b + 2), 2 * TERMS * 16, d))
                    i = 0
                    for qk, kind in ((0, "qrot"), (1, "krot")):
                        wait(pool, misc_emptied, use_no(b, kind, 2, d) + 1)
                        a, r = rope_a[:, qk, :], rest[:, qk, :]
                        link(nc.gpsimd.tensor_tensor(a, a, rope_b[:, qk, :], ALU.add), base, i + 1, d)
                        link(nc.gpsimd.tensor_copy(parts[:, qk, 0, :], a), base, i + 2, d)
                        link(nc.gpsimd.tensor_tensor(r, a, parts[:, qk, 0, :], ALU.subtract), base, i + 3, d)
                        link(nc.gpsimd.tensor_copy(parts[:, qk, 1, :], r), base, i + 4, d)
                        last = nc.gpsimd.tensor_tensor(parts[:, qk, 2, :], r, parts[:, qk, 1, :], ALU.subtract)
                        if qk == 0:
                            link(last, base, i + 5, d)
                        i += 5
                    last.then_inc(parts_made, 1)

            pipeline(pool, step)

            wait(pool, xnT_kept, B)
            def stage(u, d):
                if d is not None:
                    wait(pool, ab_made, E * (d - 1 + u))
                src = xnT_all[:, bass.ds((u if d is None else d + u) * P, P)]
                nc.gpsimd.tensor_copy(xcur[u][:], src).then_inc(xcur_made, 1)

            stage(0, None)
            stage(1, None)
            with pool.Fori(1, TILES // 2) as it:
                stage(0, it * 2)
                stage(1, it * 2)


INS = ["x", "w_q", "w_k", "w_v", "w_o", "w_g", "w1", "w2", "w3", "cos_t", "sin_t"]


def kernel(L0_attn_x, L0_attn_W_Q, L0_attn_W_K, L0_attn_W_V, L0_attn_W_O, L0_ffn_Wg, L0_ffn_W1, L0_ffn_W2, L0_ffn_W3):
    import numpy as np
    import concourse.bacc as bacc
    from concourse.bass_utils import run_bass_kernel_spmd

    inv = np.float32(1.0) / np.float32(10000.0) ** (np.arange(0, HD, 2, dtype=np.float32) / np.float32(HD))
    angle = np.outer(inv, np.arange(L, dtype=np.float32)).astype(np.float32)
    cos_t = np.repeat(np.cos(angle), 2 * H, axis=0).astype(np.float32)
    sin_t = np.repeat(np.sin(angle), 2 * H, axis=0).astype(np.float32)

    def lay(a, *axes):
        return np.ascontiguousarray(np.transpose(np.asarray(a), axes))

    def by_dimension(w):
        return lay(np.asarray(w).reshape(H, HD, D), 2, 1, 0).reshape(D, D)

    arrays = dict(x=np.ascontiguousarray(L0_attn_x), w_q=by_dimension(L0_attn_W_Q), w_k=by_dimension(L0_attn_W_K),
                  w_v=lay(L0_attn_W_V, 1, 0), w_o=lay(L0_attn_W_O, 1, 0), w_g=lay(L0_ffn_Wg, 1, 0),
                  w1=lay(L0_ffn_W1, 2, 0, 1), w2=lay(L0_ffn_W2, 2, 0, 1), w3=lay(L0_ffn_W3, 2, 0, 1),
                  cos_t=cos_t, sin_t=sin_t)
    nc = bacc.Bacc("TRN2", target_bir_lowering=False, num_devices=1)
    args = [nc.dram_tensor(f"in_{n}", arrays[n].shape, F32, kind="ExternalInput").ap() for n in INS]
    out = nc.dram_tensor("out", (B, L, D), F32, kind="ExternalOutput").ap()
    block_kernel(nc, *args, out)
    r = run_bass_kernel_spmd(nc, [{f"in_{n}": arrays[n] for n in INS}], core_ids=[0])
    return r.results[0]["out"]
```

```python
from contextlib import ExitStack

import concourse.bass as bass
from concourse import mybir

F32 = mybir.dt.float32
BF16 = mybir.dt.bfloat16
I32 = mybir.dt.int32
ALU = mybir.AluOpType
ACT = mybir.ActivationFunctionType
AX = mybir.AxisListType

P = 128
B, L, D = 8, 512, 128
H, HD = 16, 8
NT = L // P
TILES = B * NT
E, HID, TOPK = 8, 352, 2
EPS = 1e-5
G = 4
GROUPS = H // G
STEPS = GROUPS * NT
PAIRS = H // 2
TERMS = 6
ROWS = 2 * TERMS * HD
MROWS = 2 * 3
Q_TERMS = [0, 1, 2, 0, 1, 0]
K_TERMS = [0, 0, 0, 1, 1, 2]
CH = [(0, 128), (128, 128), (256, 96)]
XT = (TOPK * TILES * P + E * (P - 1)) // P
XT += -XT % 4
ROW = D + 1

USES = [
    (1, "A", "maxT", 1), (2, "A", "ctxT", -1), (3, "A", "ctxnT", -1), (4, "A", "out", -1),
    (5, "A", "maxT", 2), (6, "A", "ctxT", 0), (7, "A", "xnT", 2),
    (8, "A", "v0", 2), (8, "B", "v1", 2), (9, "A", "maxT", 3), (10, "A", "ctxT", 1), (10, "B", "q", 2),
    (11, "A", "qrot", 2), (11, "B", "k", 2), (12, "A", "krot", 2), (13, "A", "maxT", 4), (14, "A", "ctxT", 2),
]
PER_BATCH = len(USES)
ROUTE = B - 3
USES.append((15, "A", "count", 0))
EXPERTS_AT = 8


def active(b, use):
    _, _, kind, rel = use
    if kind in ("maxT", "ctxT"):
        return 0 <= GROUPS * b + rel < GROUPS * B
    if kind == "count":
        return b == ROUTE
    return 0 <= b + rel < B


ORDER = {}
for _b in range(-2, B + 1):
    for _u in USES:
        if active(_b, _u):
            ORDER[(_b, _u[2], _u[3])] = len(ORDER)


def at(base, slope, d):
    return base + slope * d if not isinstance(d, int) else base + slope * d


def block_kernel(nc, x, w_q, w_k, w_v, w_o, w_g, w1, w2, w3, cos_t, sin_t, out):
    with ExitStack() as ctx:
        def sb(name, shape, dt=F32):
            return ctx.enter_context(nc.sbuf_tensor(name, shape, dt))

        def sem(name):
            return ctx.enter_context(nc.semaphore(name))

        ps = ctx.enter_context(nc.psum_tensor("ps", [P, 8, 512], F32))
        ps_s = ps[:, 0:2, :]
        ps_m = ps[:, 2:6, :]
        ps_ctx = ps[:, 6, :]
        ps_misc = ps[:, 7, :]

        x_sb = sb("x_sb", [P, TILES, D])
        rows = sb("rows", [P, TILES, ROW])
        logits = sb("logits", [P, E, TILES])
        wqT, wkT = sb("wqT", [P, D]), sb("wkT", [P, D])
        wqr, wkr = sb("wqr", [P, D]), sb("wkr", [P, D])
        wvg = sb("wvg", [P, D + E])
        woT = sb("woT", [P, D])
        cos_sb, sin_sb = sb("cos_sb", [P, L]), sb("sin_sb", [P, L])
        ident = sb("ident", [P, P])
        ident_bf = sb("ident_bf", [P, P], BF16)
        w1_sb = sb("w1_sb", [P, E, HID])
        w3_sb = sb("w3_sb", [P, E, HID])
        w2_sb = sb("w2_sb", [P, E, 3, D])
        stats = sb("stats", [P, TILES, 6])
        mv = sb("mv", [P, TILES, 2])
        var, root, rstd = sb("var", [P, TILES]), sb("root", [P, TILES]), sb("rstd", [P, TILES])
        xn = sb("xn", [P, NT, D])
        xnT = sb("xnT", [P, L])
        v_stage = sb("v_stage", [P, NT, D])
        v_st = [sb(f"v_st{i}", [P, NT, H, 32]) for i in range(2)]
        rope_a, rope_b = sb("rope_a", [P, 2, L]), sb("rope_b", [P, 2, L])
        rest = sb("rest", [P, 2, L])
        parts = sb("parts", [P, 2, 3, L], BF16)
        q_st = [sb(f"q_st{i}", [P, PAIRS, L], BF16) for i in range(2)]
        k_st = [sb(f"k_st{i}", [P, H, L], BF16) for i in range(2)]
        negm = sb("negm", [P, 2, NT, G])
        mrest = sb("mrest", [P, NT, G])
        msplit = sb("msplit", [P, NT, G, 3], BF16)
        mrow = sb("mrow", [G * 3, L], BF16)
        probs = sb("probs", [P, 8, L])
        ctx_sb = sb("ctx_sb", [P, L])
        ctx_r = sb("ctx_r", [P, NT, G])
        ctxn = sb("ctxn", [P, NT, D])
        ctxnT = sb("ctxnT", [P, L])
        r_e, r_s, r_eq = sb("r_e", [P, E, TILES]), sb("r_s", [P, E, TILES]), sb("r_eq", [P, E, TILES])
        r_first, r_second = sb("r_first", [P, E, TILES]), sb("r_second", [P, E, TILES])
        r_top = sb("r_top", [P, 2, TILES])
        r_at = sb("r_at", [P, TILES])
        r_sum = sb("r_sum", [P, TILES])
        r_w = sb("r_w", [P, 2, TILES])
        r_mask = sb("r_mask", [P, E, TILES], BF16)
        r_cum = sb("r_cum", [P, E, TILES])
        r_zero = sb("r_zero", [P, E * TILES])
        cum_e = sb("cum_e", [P, E + 1])
        n_e, tl_e, tinc_e, off_e = (sb(n, [P, E]) for n in ("n_e", "tl_e", "tinc_e", "off_e"))
        r_cmp = sb("r_cmp", [P, E, TILES])
        ex_cmp = sb("ex_cmp", [1, XT, E - 1])
        ex_f = sb("ex_f", [1, XT])
        ex_i = sb("ex_i", [1, XT], I32)
        slot_f, slot = sb("slot_f", [P, 2, TILES]), sb("slot", [P, 2, TILES], I32)
        io_i = sb("io_i", [P, XT], I32)
        io_e = sb("io_e", [P, E])
        io_n = sb("io_n", [P, TILES])
        io_x = sb("io_x", [P, XT])
        dest = sb("dest", [P, TILES], I32)
        before = sb("before", [P, P], BF16)
        ones_bf = sb("ones_bf", [P, P], BF16)
        blank = sb("blank", [P, 8, ROW])
        xt = [sb(f"xt{i}", [P, ROW]) for i in range(4)]
        xT = [xn[:, i, :] for i in range(2)]
        gate = [rest[:].rearrange("p k l -> p (k l)")[:, HID * i:HID * (i + 1)] for i in range(2)]
        flat = parts[:].rearrange("p k t l -> p (k t l)").bitcast(F32)
        hid = [flat[:, HID * i:HID * (i + 1)] for i in range(2)]
        hidT = [flat[:, 2 * HID + 3 * P * i:2 * HID + 3 * P * (i + 1)].rearrange("p (c n) -> p c n", c=3)
                for i in range(2)]
        y_sb = [v_stage[:, i, :] for i in range(4)]
        y_to = [sb(f"y_to{i}", [P, 1], I32) for i in range(4)]
        y_in = [a[:].rearrange("p k (t d) -> p k t d", t=NT) for a in (rope_a, rope_b)]

        slots = nc.dram_tensor("slots", (XT * P, ROW), F32).ap()
        results = nc.dram_tensor("results", (2 * TILES * P + 8 * P, D), F32).ap()

        q_dram = nc.dram_tensor("q_terms", (2, 2, TERMS, HD * H, L), BF16).ap()

        x_first, x_rest, w_loaded, ffn_w_loaded = sem("x_first"), sem("x_rest"), sem("w_loaded"), sem("ffn_w_loaded")
        consts = sem("consts")
        rot_made = sem("rot_made")
        scores_made, probs_made = sem("scores_made"), sem("probs_made")
        pv_done, ctx_copied = sem("pv_done"), sem("ctx_copied")
        max_scores, max_found = sem("max_scores"), sem("max_found")
        max_split, max_rows = sem("max_split"), sem("max_rows")
        misc_filled, misc_emptied = sem("misc_filled"), sem("misc_emptied")
        xn_made, v_placed, parts_made = sem("xn_made"), sem("v_placed"), sem("parts_made")
        terms_written, stacks_loaded = sem("terms_written"), sem("stacks_loaded")
        rows_kept = sem("rows_kept")
        dve_seq, pool_seq, stat_seq, r_seq = sem("dve_seq"), sem("pool_seq"), sem("stat_seq"), sem("r_seq")
        var_made, root_made = sem("var_made"), sem("root_made")
        blank_made, iotas_made, slots_blank = sem("blank_made"), sem("iotas_made"), sem("slots_blank")
        r_shift, r_exp, r_chosen, routed = sem("r_shift"), sem("r_exp"), sem("r_chosen"), sem("routed")
        first_sent, second_sent, dest_moved = sem("first_sent"), sem("second_sent"), sem("dest_moved")
        xt_loaded = [sem(f"xt_loaded{i}") for i in range(4)]
        y_sent = [sem(f"y_sent{i}") for i in range(4)]
        xT_made, xT_copied, up_done = sem("xT_made"), sem("xT_copied"), sem("up_done")
        gate_made, hid_made = sem("gate_made"), sem("hid_made")
        hT_made, hidT_copied, y_made, y_copied = sem("hT_made"), sem("hidT_copied"), sem("y_made"), sem("y_copied")
        y_loaded = [sem(f"y_loaded{i}") for i in range(2)]
        combined = sem("combined")
        stored = sem("stored")

        block = ctx.enter_context(nc.Block())
        x_dram = x.rearrange("b (t p) d -> b p t d", p=P)
        out_dram = out.rearrange("b (t p) d -> b p t d", p=P)

        def wait(eng, semaphore, value):
            if not isinstance(value, int):
                value = eng.to_reg(value)
                eng.wait_ge(x_first, 16)
            eng.wait_ge(semaphore, value)

        def use_no(b, kind, rel, d):
            return at(ORDER[(b, kind, rel)], PER_BATCH, d)

        def uses(b, s, slot):
            return [u for u in USES if u[0] == s and u[1] == slot and active(b, u)]

        def pipeline(eng, step, experts):
            for b in (-2, -1):
                for s in range(STEPS):
                    step(b, s, 0)
            for s in range(5):
                step(0, s, 0)
            with eng.Fori(0, (ROUTE - 1) // 2) as it:
                for u in (0, 1):
                    for s in range(5, STEPS):
                        step(u, s, it * 2)
                    for s in range(5):
                        step(u + 1, s, it * 2)
            for b in range(ROUTE - 1, B):
                for s in range(5 if b == ROUTE - 1 else 0, STEPS):
                    step(b, s, 0)
                    if (b, s) == (B - 1, EXPERTS_AT):
                        experts()
            for s in range(5):
                step(B, s, 0)

        def expert_loop(eng, tile, drain):
            for j in range(4):
                tile(j, 0)
            with eng.Fori(1, XT // 4) as it:
                for j in range(4):
                    tile(j, it * 4)
            drain()

        @block.sync
        def _(sp):
            sp.dma_start(x_sb[:, 0:NT, :], x_dram[0]).then_inc(x_first, 16)
            for src, dst in ((w_q, wqT[:]), (w_k, wkT[:]), (w_v, wvg[:, 0:D]), (w_g, wvg[:, D:D + E]), (w_o, woT[:]),
                             (cos_t, cos_sb[:]), (sin_t, sin_sb[:])):
                sp.dma_start(dst, src).then_inc(w_loaded, 16)
            for b in range(1, B):
                sp.dma_start(x_sb[:, NT * b:NT * (b + 1), :], x_dram[b]).then_inc(x_rest, 16)
            wait(sp, blank_made, 1)
            for j in range(0, XT, 8):
                sp.dma_start(slots[j * P:(j + 8) * P].rearrange("(t p) n -> p t n", p=P), blank[:]
                             ).then_inc(slots_blank, 16)
            sp.dma_start(w1_sb[:], w1).then_inc(ffn_w_loaded, 16)
            sp.dma_start(w3_sb[:], w3).then_inc(ffn_w_loaded, 16)
            for c, (h0, n) in enumerate(CH):
                sp.dma_start(w2_sb[0:n, :, c, :], w2[h0:h0 + n]).then_inc(ffn_w_loaded, 16)

            def step(b, s, d):
                par = (b + 1) % 2
                if s == 0 and 0 <= b + 1 < B:
                    wait(sp, parts_made, at(b + 2, 1, d))
                    if b + 1 >= 1:
                        wait(sp, stacks_loaded, at(4 * 16 * (b + 1), 64, d))
                    for qk, terms in enumerate((Q_TERMS, K_TERMS)):
                        for t, part in enumerate(terms):
                            sp.dma_start(q_dram[par, qk, t], parts[:, qk, part, :]).then_inc(terms_written, 16)
                if s == 2 and 0 <= b + 1 < B:
                    wait(sp, terms_written, at(2 * TERMS * 16 * (b + 2), 2 * TERMS * 16, d))
                    if b + 1 >= 2:
                        wait(sp, scores_made, at(4 * STEPS * b, 4 * STEPS, d))
                    for qk in (0, 1):
                        for hh in (0, 1):
                            r0 = hh * TERMS * HD
                            src = q_dram[par, qk].rearrange("t (d p two) l -> two (t d) p l", two=2, d=HD)[hh]
                            dst = q_st[par][r0:r0 + TERMS * HD, :, :] if qk == 0 else \
                                k_st[par][r0:r0 + TERMS * HD, hh:H:2, :]
                            sp.dma_start(dst, src).then_inc(stacks_loaded, 16)
                for u in USES:
                    if u[0] == s and u[2] == "maxT" and active(b, u):
                        grp, n = GROUPS * b + u[3], use_no(b, "maxT", u[3], d)
                        wait(sp, misc_emptied, n + 1)
                        pb = (b + u[3] // GROUPS) % 2
                        for pr in range(G // 2):
                            sp.dma_start(q_st[pb][ROWS:ROWS + MROWS, 2 * (u[3] % GROUPS) + pr, :],
                                         mrow[MROWS * pr:MROWS * (pr + 1), :]).then_inc(max_rows, 16)

                if (b, s) == (B - 1, EXPERTS_AT + 1):
                    for r in range(4):
                        wait(sp, y_sent[r], 16 * XT // 4)
                    load_results(0)
                    load_results(1)
                c = STEPS * (b - B + 1) + s - EXPERTS_AT - 2
                if 0 <= c < B:
                    wait(sp, combined, c + 1)
                    if c + 2 < B:
                        load_results(c + 2)
                    if c < B - 1:
                        sp.dma_start(out_dram[c], x_sb[:, NT * c:NT * (c + 1), :]).then_inc(stored, 16)

            def load_results(c):
                for k in (0, 1):
                    src = results[(k * TILES + NT * c) * P:(k * TILES + NT * (c + 1)) * P]
                    sp.dma_start(y_in[c % 2][:, k], src.rearrange("(t p) d -> p t d", p=P)
                                 ).then_inc(y_loaded[c % 2], 16)

            def experts():
                wait(sp, second_sent, 16 * TILES)

                def tile(j, d):
                    if not (isinstance(d, int) and j < 4):
                        wait(sp, xT_copied, d + (j - 3))
                    r = j % 4
                    sp.dma_start(xt[r][:], slots[bass.ds((d + j) * P, P), :]).then_inc(xt_loaded[r], 16)

                expert_loop(sp, tile, lambda: None)

            pipeline(sp, step, experts)
            wait(sp, misc_emptied, len(ORDER))
            c = B - 1
            sp.dma_start(out_dram[c], x_sb[:, NT * c:NT * (c + 1), :]).then_inc(stored, 16)
            sp.wait_ge(stored, 16 * B)

        @block.tensor
        def _(pe):
            pe.wait_ge(w_loaded, 7 * 16)
            pe.wait_ge(consts, 3)
            pe.wait_ge(rot_made, 1)

            def shared(b, u, d):
                kind, rel = u[2], u[3]
                n = use_no(b, kind, rel, d)
                if ORDER[(b, kind, rel)] > 0:
                    pe.wait_ge(misc_emptied, n)
                if kind == "maxT":
                    pe.wait_ge(max_split, at(GROUPS * b + rel + 1, GROUPS, d))
                    dst = ps_misc.bitcast(BF16)
                    for qb in range(NT):
                        last = nc.tensor.transpose(dst[0:3 * G, qb * P:(qb + 1) * P],
                                                   msplit[:, qb].rearrange("p g t -> p (g t)"), ident_bf[:])
                elif kind == "ctxT":
                    pe.wait_ge(ctx_copied, at(GROUPS * b + rel + 1, GROUPS, d))
                    for qb in range(NT):
                        last = nc.tensor.transpose(ps_misc[:, qb * P:(qb + 1) * P],
                                                   ctx_sb[:, qb * P:(qb + 1) * P], ident[:])
                elif kind == "ctxnT":
                    for qb in range(NT):
                        last = nc.tensor.transpose(ps_misc[:, qb * P:(qb + 1) * P], ctxn[:, qb, :], ident[:])
                elif kind == "out":
                    for qb in range(NT):
                        last = nc.tensor.matmul(ps_misc[:, qb * P:(qb + 1) * P], ctxnT[:, qb * P:(qb + 1) * P],
                                                woT[:], start=True, stop=True)
                elif kind == "xnT":
                    pe.wait_ge(xn_made, at(b + rel + 1, 1, d))
                    for t in range(NT):
                        last = nc.tensor.transpose(ps_misc[:, t * P:(t + 1) * P], xn[:, t, :], ident[:])
                elif kind == "count":
                    pe.wait_ge(r_chosen, 1)
                    m = r_mask[:].rearrange("p e t -> p (e t)")
                    nc.tensor.matmul(ps_misc[:, 0:E * TILES], before[:], m, start=True, stop=True)
                    last = nc.tensor.matmul(ps_misc[:, E * TILES:2 * E * TILES], ones_bf[:], m, start=True, stop=True)
                elif kind in ("v0", "v1"):
                    t0 = 2 * int(kind[1])
                    for t in (0, 1):
                        last = nc.tensor.matmul(ps_misc[:, t * (D + E):(t + 1) * (D + E)],
                                                xnT[:, (t0 + t) * P:(t0 + t + 1) * P], wvg[:], start=True, stop=True)
                else:
                    w = {"q": wqT, "qrot": wqr, "k": wkT, "krot": wkr}[kind]
                    last = nc.tensor.matmul(ps_misc[:], w[:], xnT[:], start=True, stop=True)
                last.then_inc(misc_filled, 1)

            def step(b, s, d):
                g, kb = s // NT, s % NT
                par, live = b % 2, 0 <= b < B
                grp = GROUPS * b + g + 2
                find = 0 <= grp < GROUPS * B
                mb, mg = (b + (g + 2) // GROUPS) % 2, (g + 2) % GROUPS
                if live and kb == 0:
                    pe.wait_ge(max_rows, at(32 * (GROUPS * b + g + 1), 32 * GROUPS, d))
                if find and s % (2 * NT) == 0 and mg == 0:
                    pe.wait_ge(stacks_loaded, at(64 * (grp // GROUPS + 1), 64, d))
                for half in (0, 1):
                    if live:
                        for j in (2 * half, 2 * half + 1):
                            n = 4 * (STEPS * b + s) + j
                            if n >= 2:
                                pe.wait_ge(probs_made, at(n - 1, 4 * STEPS, d))
                            h = G * g + j
                            nc.tensor.matmul(ps_s[:, j % 2, :],
                                             k_st[par][0:ROWS + MROWS, h, kb * P:(kb + 1) * P],
                                             q_st[par][0:ROWS + MROWS, h // 2, :],
                                             start=True, stop=True).then_inc(scores_made, 1)
                    if find:
                        h = G * mg + kb
                        m = 2 * (NT * grp + kb) + half
                        if m >= 2:
                            pe.wait_ge(max_found, at(m - 1, 2 * STEPS, d))
                        for i in (0, 1):
                            qb = 2 * half + i
                            last = nc.tensor.matmul(ps_m[:, 2 * half + i, :],
                                                    q_st[mb][0:ROWS, h // 2, qb * P:(qb + 1) * P],
                                                    k_st[mb][0:ROWS, h, :], start=True, stop=True)
                        last.then_inc(max_scores, 1)
                for u in uses(b, s, "A"):
                    shared(b, u, d)
                n = STEPS * b + s - 1
                if 0 <= n < STEPS * B:
                    pb, ps_ = (b if s else b - 1) % 2, (s - 1) % STEPS
                    pg, pk = ps_ // NT, ps_ % NT
                    pe.wait_ge(probs_made, at(4 * (n + 1), 4 * STEPS, d))
                    if pk == 0 and n >= NT:
                        pe.wait_ge(ctx_copied, at(n // NT, GROUPS, d))
                    if pk == 0 and pg == 0:
                        pe.wait_ge(v_placed, at(n // STEPS + 1, 1, d))
                    for j in range(G):
                        last = nc.tensor.matmul(ps_ctx[32 * j:32 * j + 32, :], v_st[pb][:, pk, G * pg + j, :],
                                                probs[:, 4 * (ps_ % 2) + j, :], start=(pk == 0), stop=(pk == NT - 1))
                    last.then_inc(pv_done, 1)
                for u in uses(b, s, "B"):
                    shared(b, u, d)

            def experts():
                pe.wait_ge(ffn_w_loaded, 5 * 16)
                pe.wait_ge(routed, 1)
                pe.wait_ge(misc_emptied, ORDER[(B - 1, "ctxT", 0)] + 1)
                pe.wait_ge(probs_made, 4 * (STEPS * (B - 1) + EXPERTS_AT + 1))
                pe.wait_ge(max_found, 2 * STEPS * B)
                pe.wait_ge(ctx_copied, GROUPS * (B - 1) + 2)

                def expert_of(j, d):
                    ap = ex_i[0:1, j:j + 1] if isinstance(d, int) else ex_i[0:1, bass.ds(d + j, 1)]
                    return pe.value_load(ap, min_val=0, max_val=E - 1)

                def turn(j, d):
                    pe.wait_ge(xt_loaded[j % 4], 16 * (j // 4 + 1) if isinstance(d, int) else d * 4 + 16 * (j // 4 + 1))
                    if not (isinstance(d, int) and j < 1):
                        pe.wait_ge(xT_copied, d + j)
                    nc.tensor.transpose(ps[:, 7, 0:P], xt[j % 4][:, 0:D], ident[:]).then_inc(xT_made, 1)

                def up(j, d):
                    e = expert_of(j, d)
                    pe.wait_ge(xT_copied, d + (j + 1))
                    if not (isinstance(d, int) and j < 2):
                        pe.wait_ge(hid_made, d + (j - 1))
                    for k, w in enumerate((w1_sb, w3_sb)):
                        last = nc.tensor.matmul(ps[:, 2 * (j % 2) + k, 0:HID], xT[j % 2],
                                                w[:, bass.ds(e, 1), :].rearrange("p a n -> p (a n)"),
                                                start=True, stop=True)
                    last.then_inc(up_done, 1)

                def turn_hidden(j, d):
                    pe.wait_ge(hid_made, d + (j + 1))
                    if not (isinstance(d, int) and j < 2):
                        pe.wait_ge(hidT_copied, 2 * d + 2 * (j - 1))
                    for i, (h0, m) in enumerate(CH):
                        last = nc.tensor.transpose(ps[0:m, 4 + j % 2, i * P:(i + 1) * P], hid[j % 2][:, h0:h0 + m],
                                                   ident[:])
                    last.then_inc(hT_made, 1)

                def down(j, d):
                    e = expert_of(j, d)
                    pe.wait_ge(hidT_copied, 2 * d + 2 * (j + 1))
                    if not (isinstance(d, int) and j < 1):
                        pe.wait_ge(y_copied, d + j)
                    for i, (h0, m) in enumerate(CH):
                        last = nc.tensor.matmul(ps[:, 6, 0:D], hidT[j % 2][0:m, i, :],
                                                w2_sb[0:m, bass.ds(e, 1), i, :].rearrange("p a n -> p (a n)"),
                                                start=(i == 0), stop=(i == 2))
                    last.then_inc(y_made, 1)

                def tile(j, d):
                    up(j, d)
                    if not (isinstance(d, int) and j < 2):
                        down(j - 2, d)
                    if not (isinstance(d, int) and j + d == XT - 1):
                        turn(j + 1, d)
                    if not (isinstance(d, int) and j < 1):
                        turn_hidden(j - 1, d)

                turn(0, 0)
                for j in range(4):
                    tile(j, 0)
                with pe.Fori(1, XT // 4 - 1) as it:
                    for j in range(4):
                        tile(j, it * 4)
                for j in range(XT - 4, XT):
                    tile(j, 0)
                down(XT - 2, 0)
                turn_hidden(XT - 1, 0)
                down(XT - 1, 0)
                pe.wait_ge(y_copied, XT)

            pipeline(pe, step, experts)

        @block.scalar
        def _(act):
            def shared(b, u, d):
                kind, rel = u[2], u[3]
                if kind not in ("maxT", "ctxnT", "xnT", "v0", "v1"):
                    return
                n = use_no(b, kind, rel, d)
                act.wait_ge(misc_filled, n + 1)
                if kind == "maxT":
                    if GROUPS * b + rel >= 1:
                        act.wait_ge(max_rows, at(32 * (GROUPS * b + rel), 32 * GROUPS, d))
                    nc.scalar.copy(mrow[:], ps_misc.bitcast(BF16)[0:3 * G, 0:L]).then_inc(misc_emptied, 1)
                elif kind == "ctxnT":
                    nc.scalar.copy(ctxnT[:], ps_misc[:]).then_inc(misc_emptied, 1)
                elif kind == "xnT":
                    nc.scalar.copy(xnT[:], ps_misc[:]).then_inc(misc_emptied, 1)
                else:
                    t0 = 2 * int(kind[1])
                    if kind == "v0" and b + rel >= 1:
                        act.wait_ge(v_placed, at(b + rel, 1, d))
                    both = ps_misc[:, 0:2 * (D + E)].rearrange("p (t n) -> p t n", t=2)
                    nc.scalar.copy(v_stage[:, t0:t0 + 2, :], both[:, :, 0:D])
                    nc.scalar.copy(logits[:, :, bass.ds(at(NT * (b + rel) + t0, NT, d), 2)],
                                   both[:, :, D:D + E].rearrange("p t e -> p e t")).then_inc(misc_emptied, 1)

            def step(b, s, d):
                live = 0 <= b < B
                if b < 0 and s == 0:
                    t0, t1 = (0, NT) if b == -2 else (NT, TILES)
                    act.wait_ge(var_made, b + 3)
                    nc.scalar.activation(root[:, t0:t1], var[:, t0:t1], ACT.Sqrt).then_inc(root_made, 1)

                def exps(j0):
                    for j in (j0, j0 + 1):
                        n = 4 * (STEPS * b + s) + j
                        if j % 4 == 0 and n >= 8:
                            act.wait_ge(pv_done, at(n // 4 - 1, STEPS, d))
                        act.wait_ge(scores_made, at(n + 1, 4 * STEPS, d))
                        nc.scalar.activation(probs[:, n % 8, :], ps_s[:, j % 2, :], ACT.Exp,
                                             scale=float(HD) ** -0.5).then_inc(probs_made, 1)

                if live:
                    exps(0)
                pb, psn = (b, s - 1) if s else (b - 1, STEPS - 1)
                for u in USES:
                    if (u[0], u[1]) == (psn, "B") and s and active(b, u):
                        shared(b, u, d)
                n = STEPS * b + s - 1
                if n >= NT and n % NT == 0 and n // NT <= GROUPS * B and (b, s) != (B - 1, EXPERTS_AT + 1):
                    copy_context(n // NT - 1, b, d)
                if live:
                    exps(2)
                for u in uses(b, s, "A"):
                    shared(b, u, d)
                if (b, s) == (B - 1, EXPERTS_AT):
                    copy_context(GROUPS * b + 1, b, d)
                if (b, s) == (ROUTE, 11):
                    act.wait_ge(r_shift, 1)
                    nc.scalar.activation(r_e[:], r_s[:], ACT.Exp).then_inc(r_exp, 1)

            def copy_context(grp, b, d):
                act.wait_ge(pv_done, at(NT * (grp + 1), STEPS, d))
                if grp >= 1:
                    act.wait_ge(misc_filled, ctx_use(grp - 1, b, d) + 1)
                nc.scalar.copy(ctx_sb[:], ps_ctx[:]).then_inc(ctx_copied, 1)

            def ctx_use(grp, b, d):
                for (bb, kind, rel), n in ORDER.items():
                    if kind == "ctxT" and GROUPS * bb + rel == grp:
                        return at(n, PER_BATCH, d)

            def experts():
                def back(j, d):
                    act.wait_ge(hT_made, d + (j + 1))
                    if not (isinstance(d, int) and j < 2):
                        act.wait_ge(y_made, d + (j - 1))
                    nc.scalar.copy(hidT[j % 2][:, 0:2, :],
                                   ps[:, 4 + j % 2, 0:2 * P].rearrange("p (c n) -> p c n", c=2))
                    nc.scalar.copy(hidT[j % 2][0:CH[2][1], 2, :],
                                   ps[0:CH[2][1], 4 + j % 2, 2 * P:3 * P]).then_inc(hidT_copied, 2)

                def tile(j, d):
                    act.wait_ge(up_done, d + (j + 1))
                    if not (isinstance(d, int) and j < 2):
                        act.wait_ge(hid_made, d + (j - 1))
                    nc.scalar.activation(gate[j % 2], ps[:, 2 * (j % 2), 0:HID], ACT.Silu).then_inc(gate_made, 1)
                    if not (isinstance(d, int) and j < 1):
                        back(j - 1, d)

                expert_loop(act, tile, lambda: back(XT - 1, 0))

            pipeline(act, step, experts)

        @block.vector
        def _(dve):
            count = [0]

            def link(ins, per=None):
                ins.then_inc(dve_seq, 1)
                return ins

            for i in (0, 1):
                nc.vector.memset(v_st[i][:], 0.0).then_inc(consts, 1)
            dve.wait_ge(w_loaded, 7 * 16)
            for src, dst in ((wqT, wqr), (wkT, wkr)):
                s2, d2 = (a[:].rearrange("p (n two h) -> p n two h", two=2, h=H) for a in (src, dst))
                nc.vector.tensor_scalar(d2[:, :, 0, :], s2[:, :, 1, :], -1.0, None, ALU.mult)
                last = nc.vector.tensor_copy(d2[:, :, 1, :], s2[:, :, 0, :])
            last.then_inc(rot_made, 1)

            seq_at, tot = {}, 2 * 4
            for bb in range(-2, B + 1):
                for u in USES:
                    if u[2] == "ctxT" and active(bb, u):
                        seq_at[("ctx", bb, u[3])] = tot
                        tot += 1
            PER = GROUPS

            def statistics(no, t0, t1):
                base = 4 * no
                for t in range(t0, t1):
                    last = nc.vector.bn_stats(stats[:, t, :], x_sb[:, t, :])
                link(last)
                dve.wait_ge(dve_seq, base + 1)
                for t in range(t0, t1):
                    last = nc.vector.bn_aggr(mv[:, t, :], stats[:, t, :])
                link(last)
                dve.wait_ge(dve_seq, base + 2)
                nc.vector.tensor_scalar(var[:, t0:t1], mv[:, t0:t1, 1], EPS, None, ALU.add).then_inc(var_made, 1)
                dve.wait_ge(root_made, no + 1)
                nc.vector.reciprocal(rstd[:, t0:t1], root[:, t0:t1]).then_inc(stat_seq, 1)
                dve.wait_ge(stat_seq, 3 * no + 1)
                link(nc.vector.tensor_tensor(rstd[:, t0:t1], var[:, t0:t1], rstd[:, t0:t1], ALU.mult))
                dve.wait_ge(dve_seq, base + 3)
                link(nc.vector.tensor_tensor(root[:, t0:t1], rstd[:, t0:t1], root[:, t0:t1], ALU.add))
                dve.wait_ge(dve_seq, base + 4)
                nc.vector.tensor_scalar(root[:, t0:t1], root[:, t0:t1], 0.5, None, ALU.mult).then_inc(stat_seq, 1)
                dve.wait_ge(stat_seq, 3 * no + 2)
                nc.vector.reciprocal(rstd[:, t0:t1], root[:, t0:t1]).then_inc(stat_seq, 1)
                dve.wait_ge(stat_seq, 3 * no + 3)

            def layer_norm(b, d):
                if b == -2:
                    dve.wait_ge(x_first, 16)
                    statistics(0, 0, NT)
                if b + 2 >= 1:
                    dve.wait_ge(misc_filled, use_no(b - 1, "xnT", 2, d) + 1)
                    dve.wait_ge(rows_kept, at(b + 2, 1, d))
                for t in range(NT):
                    nt = bass.ds(at(NT * (b + 2) + t, NT, d), 1)
                    last = nc.vector.tensor_scalar(xn[:, t, :], x_sb[:, nt, :].rearrange("p a n -> p (a n)"),
                                                   mv[:, nt, 0], rstd[:, nt], ALU.subtract, ALU.mult)
                last.then_inc(xn_made, 1)

            def shared(b, u, d):
                kind, rel = u[2], u[3]
                if kind in ("maxT", "ctxnT", "xnT", "v0", "v1"):
                    return
                n = use_no(b, kind, rel, d)
                dve.wait_ge(misc_filled, n + 1)
                if kind == "ctxT":
                    g = (GROUPS + rel) % GROUPS
                    t4 = ps_misc.rearrange("p (q j c) -> p q j c", q=NT, j=G)
                    link(nc.vector.reciprocal(ctx_r[:], t4[:, :, :, HD]))
                    dve.wait_ge(dve_seq, at(seq_at[("ctx", b, rel)] + 1, PER, d))
                    nc.vector.tensor_tensor(
                        ctxn[:, :, g * G * HD:(g + 1) * G * HD].rearrange("p q (j c) -> p q j c", j=G),
                        t4[:, :, :, 0:HD], ctx_r[:].rearrange("p q (j one) -> p q j one", one=1).to_broadcast(
                            [P, NT, G, HD]), ALU.mult).then_inc(misc_emptied, 1)
                elif kind == "out":
                    sl = x_sb[:, bass.ds(at(NT * (b + rel), NT, d), NT), :]
                    if b + rel == B - 1:
                        dve.wait_ge(combined, B)
                    nc.vector.tensor_tensor(sl, ps_misc.rearrange("p (t n) -> p t n", t=NT), sl,
                                            ALU.add).then_inc(misc_emptied, 1)
                elif kind == "count":
                    place()
                else:
                    if kind == "q" and b + rel >= 1:
                        dve.wait_ge(parts_made, at(b + rel, 1, d))
                    dst = (rope_a if kind in "qk" else rope_b)[:, 0 if kind[0] == "q" else 1, :]
                    nc.vector.tensor_tensor(dst, ps_misc[:], (cos_sb if kind in "qk" else sin_sb)[:],
                                            ALU.mult).then_inc(misc_emptied, 1)

            def step(b, s, d):
                g, kb = s // NT, s % NT
                grp = GROUPS * b + g + 2
                if 0 <= grp < GROUPS * B:
                    if kb == 0 and grp >= 2:
                        dve.wait_ge(max_split, at(grp - 1, GROUPS, d))
                    for half in (0, 1):
                        m = 2 * (NT * grp + kb) + half
                        dve.wait_ge(max_scores, at(m + 1, 2 * STEPS, d))
                        nc.vector.tensor_reduce(negm[:, g % 2, 2 * half:2 * half + 2, kb],
                                                ps_m[:, 2 * half:2 * half + 2, :], axis=AX.X, op=ALU.max,
                                                negate=True).then_inc(max_found, 1)
                if s == 0 and b == -1:
                    dve.wait_ge(x_rest, 16 * (B - 1))
                    statistics(1, NT, TILES)
                if s == 5 and 0 <= b + 2 < B:
                    layer_norm(b, d)
                if (b, s) == (ROUTE, 10):
                    shift_logits()
                if (b, s) == (ROUTE, 12):
                    scores()
                if b == ROUTE and s in (13, 14):
                    choose(s - 13)
                for slot_ in "AB":
                    for u in uses(b, s, slot_):
                        shared(b, u, d)
                if (b, s) == (ROUTE + 1, 0):
                    place_rows()
                c = STEPS * (b - B + 1) + s - EXPERTS_AT - 2
                if 0 <= c < B:
                    combine(c)

            chain = [0]

            def then(ins):
                chain[0] += 1
                ins.then_inc(r_seq, 1)
                dve.wait_ge(r_seq, chain[0])

            def by_tile(a):
                return a.rearrange("p e t -> p t e")

            def over_e(a, n=E):
                return a.rearrange("p (one t) -> p one t", one=1).to_broadcast([P, n, TILES])

            def over_t(a):
                return a.rearrange("p (e one) -> p e one", one=1).to_broadcast([P, E, TILES])

            def shift_logits():
                dve.wait_ge(misc_emptied, ORDER[(ROUTE, "v1", 2)] + 1)
                then(nc.vector.tensor_reduce(r_sum[:], by_tile(logits[:]), axis=AX.X, op=ALU.max))
                nc.vector.tensor_tensor(r_s[:], logits[:], over_e(r_sum[:]), ALU.subtract).then_inc(r_shift, 1)

            def scores():
                dve.wait_ge(r_exp, 1)
                then(nc.vector.tensor_reduce(r_sum[:], by_tile(r_e[:]), axis=AX.X, op=ALU.add))
                then(nc.vector.reciprocal(r_sum[:], r_sum[:]))
                then(nc.vector.tensor_tensor(r_s[:], r_e[:], over_e(r_sum[:]), ALU.mult))

            def choose(k):
                if k == 0:
                    dve.wait_ge(iotas_made, 1)
                one_hot = (r_first, r_second)[k]
                then(nc.vector.tensor_reduce(r_top[:, k, :], by_tile(r_s[:]), axis=AX.X, op=ALU.max))
                then(nc.vector.tensor_tensor(r_eq[:], r_s[:], over_e(r_top[:, k, :]), ALU.is_equal))
                then(nc.vector.tensor_tensor(r_eq[:], r_eq[:], over_t(io_e[:]), ALU.mult))
                then(nc.vector.tensor_reduce(r_at[:], by_tile(r_eq[:]), axis=AX.X, op=ALU.min))
                then(nc.vector.tensor_tensor(one_hot[:], over_t(io_e[:]), over_e(r_at[:]), ALU.is_equal))
                if k == 0:
                    then(nc.vector.scalar_tensor_tensor(r_s[:], r_first[:], -4.0, r_s[:], op0=ALU.mult, op1=ALU.add))
                else:
                    nc.vector.tensor_tensor(r_mask[:], r_first[:], r_second[:], ALU.add).then_inc(r_chosen, 1)

            def place():
                total = ps_misc[:, E * TILES:2 * E * TILES]
                flat = r_cum[:].rearrange("p e t -> p (e t)")
                then(nc.vector.tensor_tensor_scan(flat, total, r_zero[:], 0.0, ALU.add, ALU.add))
                then(nc.vector.tensor_copy(cum_e[:, 1:E + 1], r_cum[:, :, TILES - 1]))
                then(nc.vector.tensor_tensor(flat, flat, total, ALU.subtract))
                nc.vector.tensor_tensor(flat, flat, ps_misc[:, 0:E * TILES], ALU.add).then_inc(misc_emptied, 1)

            def place_rows():
                then(nc.vector.tensor_tensor(n_e[:], cum_e[:, 1:E + 1], cum_e[:, 0:E], ALU.subtract))
                then(nc.vector.tensor_tensor(r_cmp[:], over_t(n_e[:]), over_e(io_n[:]), ALU.is_gt))
                then(nc.vector.tensor_reduce(tl_e[:], r_cmp[:], axis=AX.X, op=ALU.add))
                then(nc.vector.tensor_tensor_scan(tinc_e[:], tl_e[:], r_zero[:, 0:E], 0.0, ALU.add, ALU.add))
                then(nc.vector.tensor_tensor(off_e[:], tinc_e[:], tl_e[:], ALU.subtract))
                then(nc.vector.scalar_tensor_tensor(off_e[:], off_e[:], float(P), cum_e[:, 0:E], op0=ALU.mult,
                                                    op1=ALU.subtract))
                dve.wait_ge(misc_emptied, ORDER[(ROUTE, "count", 0)] + 1)
                then(nc.vector.tensor_tensor(r_cum[:], r_cum[:], over_t(off_e[:]), ALU.add))
                for k, one_hot in ((0, r_first), (1, r_second)):
                    then(nc.vector.tensor_tensor(r_cmp[:], one_hot[:], r_cum[:], ALU.mult))
                    then(nc.vector.tensor_reduce(slot_f[:, k, :], by_tile(r_cmp[:]), axis=AX.X, op=ALU.add))
                then(nc.vector.tensor_copy(slot[:], slot_f[:]))
                then(nc.vector.tensor_tensor(
                    ex_cmp[:], io_x[0:1, :].rearrange("p (x one) -> p x one", one=1).to_broadcast([1, XT, E - 1]),
                    tinc_e[0:1, 0:E - 1].rearrange("p (one e) -> p one e", one=1).to_broadcast([1, XT, E - 1]),
                    ALU.is_ge))
                then(nc.vector.tensor_reduce(ex_f[:], ex_cmp[:], axis=AX.X, op=ALU.add))
                nc.vector.tensor_copy(ex_i[:], ex_f[:]).then_inc(routed, 1)
                then(nc.vector.tensor_tensor(r_sum[:], r_top[:, 0, :], r_top[:, 1, :], ALU.add))
                then(nc.vector.tensor_scalar(r_sum[:], r_sum[:], 1e-20, None, ALU.add))
                then(nc.vector.reciprocal(r_sum[:], r_sum[:]))
                for k in (0, 1):
                    then(nc.vector.tensor_tensor(r_w[:, k, :], r_top[:, k, :], r_sum[:], ALU.mult))

            def combine(c):
                dve.wait_ge(y_loaded[c % 2], 32 * (c // 2 + 1))
                dve.wait_ge(misc_emptied, ORDER[(B - 1, "out", -1)] + 1)
                for k in (0, 1):
                    for t in range(NT):
                        sl = x_sb[:, NT * c + t, :]
                        last = nc.vector.scalar_tensor_tensor(sl, y_in[c % 2][:, k, t, :],
                                                              r_w[:, k, NT * c + t:NT * c + t + 1], sl,
                                                              op0=ALU.mult, op1=ALU.add)
                    if k == 0:
                        then(last)
                last.then_inc(combined, 1)

            def experts():
                def copy_xT(j, d):
                    dve.wait_ge(xT_made, d + (j + 1))
                    if not (isinstance(d, int) and j < 4):
                        dve.wait_ge(y_sent[j % 4], d * 4 + 16 * (j // 4))
                    nc.vector.tensor_copy(y_to[j % 4][:], xt[j % 4][:, D:D + 1].bitcast(I32))
                    if not (isinstance(d, int) and j < 2):
                        dve.wait_ge(up_done, d + (j - 1))
                    nc.vector.tensor_copy(xT[j % 2], ps[:, 7, 0:P]).then_inc(xT_copied, 1)

                def copy_y(j, d):
                    dve.wait_ge(y_made, d + (j + 1))
                    if not (isinstance(d, int) and j < 4):
                        dve.wait_ge(y_sent[j % 4], d * 4 + 16 * (j // 4))
                    nc.vector.tensor_copy(y_sb[j % 4], ps[:, 6, 0:D]).then_inc(y_copied, 1)

                def tile(j, d):
                    if not (isinstance(d, int) and j < 2):
                        copy_y(j - 2, d)
                    if not (isinstance(d, int) and j + d == XT - 1):
                        copy_xT(j + 1, d)
                    dve.wait_ge(gate_made, d + (j + 1))
                    if not (isinstance(d, int) and j < 2):
                        dve.wait_ge(hT_made, d + (j - 1))
                    nc.vector.tensor_tensor(hid[j % 2], gate[j % 2], ps[:, 2 * (j % 2) + 1, 0:HID],
                                            ALU.mult).then_inc(hid_made, 1)

                copy_xT(0, 0)
                for j in range(4):
                    tile(j, 0)
                with dve.Fori(1, XT // 4 - 1) as it:
                    for j in range(4):
                        tile(j, it * 4)
                for j in range(XT - 4, XT):
                    tile(j, 0)
                copy_y(XT - 2, 0)
                copy_y(XT - 1, 0)

            nc.vector.memset(r_zero[:], 0.0)
            nc.vector.memset(ones_bf[:], 1.0)
            then(nc.vector.memset(cum_e[:, 0:1], 0.0))
            pipeline(dve, step, experts)

        @block.gpsimd
        def _(pool):
            made = [0]

            def then(ins):
                made[0] += 1
                ins.then_inc(pool_seq, 1)
                pool.wait_ge(pool_seq, made[0])

            then(nc.gpsimd.memset(ident[:], 0.0))
            then(nc.gpsimd.affine_select(out=ident[:], in_=ident[:], compare_op=ALU.not_equal, fill=1.0, base=0,
                                         pattern=[[-1, P]], channel_multiplier=1))
            then(nc.gpsimd.tensor_copy(ident_bf[:], ident[:]))
            for i in (0, 1):
                then(nc.gpsimd.memset(k_st[i][:], 0.0))
                for hh, base, sign in ((0, 2, -1), (1, -3, 1)):
                    v = k_st[i][ROWS:P, hh:H:2, :]
                    then(nc.gpsimd.memset(v, 1.0))
                    then(nc.gpsimd.affine_select(out=v, in_=v, compare_op=ALU.is_ge, fill=0.0, base=base,
                                                 pattern=[[0, PAIRS], [0, L]], channel_multiplier=sign))
            then(nc.gpsimd.memset(before[:], 1.0))
            then(nc.gpsimd.affine_select(out=before[:], in_=before[:], compare_op=ALU.is_gt, fill=0.0, base=0,
                                         pattern=[[1, P]], channel_multiplier=-1))
            pool.wait_ge(consts, 2)
            for i in (0, 1):
                last = nc.gpsimd.memset(v_st[i][:, :, :, HD:HD + 1], 1.0)
            last.then_inc(consts, 1)
            for n, base, step_, mult, dst in ((E, -E, 1, 0, io_e), (TILES, 0, P, 0, io_n), (XT, 0, 1, 0, io_x)):
                then(nc.gpsimd.iota(io_i[:, 0:n], pattern=[[step_, n]], base=base, channel_multiplier=mult))
                then(nc.gpsimd.tensor_copy(dst[:], io_i[:, 0:n]))
            then(nc.gpsimd.iota(dest[:], pattern=[[P, TILES]], base=0, channel_multiplier=1))
            then(nc.gpsimd.tensor_copy(rows[:, :, D].bitcast(I32), dest[:]))
            then(nc.gpsimd.memset(blank[:], 0.0))
            then(nc.gpsimd.iota(blank[:, :, D].bitcast(I32), pattern=[[P, 8]], base=2 * TILES * P,
                                channel_multiplier=1))
            nc.gpsimd.memset(io_i[:], 0).then_inc(iotas_made, 1)
            pool.wait_ge(iotas_made, 1)
            nc.gpsimd.tensor_copy(io_i[:], io_i[:]).then_inc(blank_made, 1)

            SENDS = STEPS + EXPERTS_AT
            M_LINKS, S_LINKS = 3, 5
            seq_at, tot = {}, made[0]
            for bb in range(-2, B + 1):
                for ss in range(STEPS):
                    if ss % NT == 0 and 0 <= GROUPS * bb + ss // NT + 1 < GROUPS * B:
                        seq_at[("m", bb, ss)] = tot
                        tot += M_LINKS
                    if ss == 12 and 0 <= bb + 2 < B:
                        seq_at[("s", bb)] = tot
                        tot += 2 * S_LINKS - 1
            PER = GROUPS * M_LINKS + 2 * S_LINKS - 1

            def link(ins, base, i, d):
                ins.then_inc(pool_seq, 1)
                wait(pool, pool_seq, at(base + i, PER, d))

            def step(b, s, d):
                g, kb = s // NT, s % NT
                grp = GROUPS * b + g + 1
                if kb == 0 and 0 <= grp < GROUPS * B:
                    base = seq_at[("m", b, s)]
                    wait(pool, max_found, at(2 * NT * (grp + 1), 2 * STEPS, d))
                    if grp >= 1:
                        bb, rel = (b, g) if g else (b - 1, GROUPS)
                        wait(pool, misc_filled, use_no(bb, "maxT", rel, d) + 1)
                    src = negm[:, (g + 1) % 2]
                    link(nc.gpsimd.tensor_copy(msplit[:, :, :, 0], src), base, 1, d)
                    link(nc.gpsimd.tensor_tensor(mrest[:], src, msplit[:, :, :, 0], ALU.subtract), base, 2, d)
                    link(nc.gpsimd.tensor_copy(msplit[:, :, :, 1], mrest[:]), base, 3, d)
                    nc.gpsimd.tensor_tensor(msplit[:, :, :, 2], mrest[:], msplit[:, :, :, 1],
                                            ALU.subtract).then_inc(max_split, 1)
                if s == 1 and 0 <= b + 1 < B:
                    wait(pool, misc_emptied, use_no(b - 1, "v1", 2, d) + 1)
                    if b >= 1:
                        wait(pool, pv_done, at(STEPS * b, STEPS, d))
                    last = None
                    for t in range(NT):
                        last = nc.gpsimd.tensor_copy(v_st[(b + 1) % 2][:, t, :, 0:HD],
                                                     v_stage[:, t, :].rearrange("p (h c) -> p h c", h=H))
                    last.then_inc(v_placed, 1)
                if s == 8 and 0 <= b + 2 < B:
                    wait(pool, xn_made, at(b + 3, 1, d))
                    nc.gpsimd.tensor_copy(rows[:, bass.ds(at(NT * (b + 2), NT, d), NT), 0:D],
                                          xn[:]).then_inc(rows_kept, 1)
                i = STEPS * (b - ROUTE - 1) + s - 1
                if 0 <= i < SENDS:
                    send(i)
                if s == 12 and 0 <= b + 2 < B:
                    base = seq_at[("s", b)]
                    if b + 2 >= 1:
                        wait(pool, terms_written, at(2 * TERMS * 16 * (b + 2), 2 * TERMS * 16, d))
                    i = 0
                    for qk, kind in ((0, "qrot"), (1, "krot")):
                        wait(pool, misc_emptied, use_no(b, kind, 2, d) + 1)
                        a, r = rope_a[:, qk, :], rest[:, qk, :]
                        link(nc.gpsimd.tensor_tensor(a, a, rope_b[:, qk, :], ALU.add), base, i + 1, d)
                        link(nc.gpsimd.tensor_copy(parts[:, qk, 0, :], a), base, i + 2, d)
                        link(nc.gpsimd.tensor_tensor(r, a, parts[:, qk, 0, :], ALU.subtract), base, i + 3, d)
                        link(nc.gpsimd.tensor_copy(parts[:, qk, 1, :], r), base, i + 4, d)
                        last = nc.gpsimd.tensor_tensor(parts[:, qk, 2, :], r, parts[:, qk, 1, :], ALU.subtract)
                        if qk == 0:
                            link(last, base, i + 5, d)
                        i += 5
                    last.then_inc(parts_made, 1)

            def send(i):
                per = -(-2 * TILES // SENDS)
                for n in range(i * per, min((i + 1) * per, 2 * TILES)):
                    k, t = n // TILES, n % TILES
                    if n == 0:
                        pool.wait_ge(routed, 1)
                        pool.wait_ge(slots_blank, 16 * (XT // 8))
                        pool.wait_ge(rows_kept, B)
                    if n == TILES:
                        pool.wait_ge(first_sent, 16 * TILES)
                        nc.gpsimd.iota(rows[:, :, D].bitcast(I32), pattern=[[P, TILES]], base=TILES * P,
                                       channel_multiplier=1).then_inc(dest_moved, 1)
                        pool.wait_ge(dest_moved, 1)
                    nc.gpsimd.indirect_dma_start(
                        out=slots, out_offset=bass.IndirectOffsetOnAxis(ap=slot[:, k, t:t + 1], axis=0),
                        in_=rows[:, t, :], in_offset=None).then_inc((first_sent, second_sent)[k], 16)

            def experts():
                def tile(j, d):
                    wait(pool, y_copied, d + (j + 1))
                    nc.gpsimd.indirect_dma_start(
                        out=results, out_offset=bass.IndirectOffsetOnAxis(ap=y_to[j % 4][:], axis=0),
                        in_=y_sb[j % 4], in_offset=None).then_inc(y_sent[j % 4], 16)

                expert_loop(pool, tile, lambda: None)

            pipeline(pool, step, experts)


INS = ["x", "w_q", "w_k", "w_v", "w_o", "w_g", "w1", "w2", "w3", "cos_t", "sin_t"]


def kernel(L0_attn_x, L0_attn_W_Q, L0_attn_W_K, L0_attn_W_V, L0_attn_W_O, L0_ffn_Wg, L0_ffn_W1, L0_ffn_W2, L0_ffn_W3):
    import numpy as np
    import concourse.bacc as bacc
    from concourse.bass_utils import run_bass_kernel_spmd

    inv = np.float32(1.0) / np.float32(10000.0) ** (np.arange(0, HD, 2, dtype=np.float32) / np.float32(HD))
    angle = np.outer(inv, np.arange(L, dtype=np.float32)).astype(np.float32)
    cos_t = np.repeat(np.cos(angle), 2 * H, axis=0).astype(np.float32)
    sin_t = np.repeat(np.sin(angle), 2 * H, axis=0).astype(np.float32)

    def lay(a, *axes):
        return np.ascontiguousarray(np.transpose(np.asarray(a), axes))

    def by_dimension(w):
        return lay(np.asarray(w).reshape(H, HD, D), 2, 1, 0).reshape(D, D)

    arrays = dict(x=np.ascontiguousarray(L0_attn_x), w_q=by_dimension(L0_attn_W_Q), w_k=by_dimension(L0_attn_W_K),
                  w_v=lay(L0_attn_W_V, 1, 0), w_o=lay(L0_attn_W_O, 1, 0), w_g=lay(L0_ffn_Wg, 1, 0),
                  w1=lay(L0_ffn_W1, 2, 0, 1), w2=lay(L0_ffn_W2, 2, 0, 1), w3=lay(L0_ffn_W3, 2, 0, 1),
                  cos_t=cos_t, sin_t=sin_t)
    nc = bacc.Bacc("TRN2", target_bir_lowering=False, num_devices=1)
    args = [nc.dram_tensor(f"in_{n}", arrays[n].shape, F32, kind="ExternalInput").ap() for n in INS]
    out = nc.dram_tensor("out", (B, L, D), F32, kind="ExternalOutput").ap()
    block_kernel(nc, *args, out)
    r = run_bass_kernel_spmd(nc, [{f"in_{n}": arrays[n] for n in INS}], core_ids=[0])
    return r.results[0]["out"]
```

```python
from contextlib import ExitStack

import concourse.bass as bass
from concourse import mybir

F32 = mybir.dt.float32
BF16 = mybir.dt.bfloat16
I32 = mybir.dt.int32
ALU = mybir.AluOpType
ACT = mybir.ActivationFunctionType
AX = mybir.AxisListType

P = 128
B, L, D = 8, 512, 128
H, HD = 16, 8
NT = L // P
TILES = B * NT
E, HID, TOPK = 8, 352, 2
EPS = 1e-5
G = 4
GROUPS = H // G
STEPS = GROUPS * NT
PAIRS = H // 2
TERMS = 6
ROWS = 2 * TERMS * HD
MROWS = 2 * 3
RUNS = [(0, 3, 0), (3, 2, 1), (5, 1, 2)]
CHUNKS = -(-HID // P)
LAST = HID - (CHUNKS - 1) * P
XT = (TOPK * TILES * P + E * (P - 1)) // P
UNROLL = 8
BLANKS = 6
SLOT_TILES = XT + -XT % (4 * BLANKS)
ROW = D + 1
POOL_COMBINES = (2, 5)
DVE_COMBINES = [c for c in range(B) if c not in POOL_COMBINES]

USES = [
    (0, "A", "xnT", 2), (1, "A", "maxT", 1), (2, "A", "ctxT", -1), (2, "B", "v0", 2), (3, "A", "ctxnT", -1),
    (4, "A", "out", -1), (4, "B", "v1", 2), (5, "A", "maxT", 2), (6, "A", "ctxT", 0), (9, "A", "maxT", 3),
    (10, "A", "ctxT", 1), (10, "B", "q", 2), (11, "A", "qrot", 2), (11, "B", "k", 2), (12, "A", "krot", 2),
    (13, "A", "maxT", 4), (14, "A", "ctxT", 2),
]
PER_BATCH = len(USES)
LOOPED = B - 4
LATE = 2
ROUTE = B - LATE - 2
USES.append((14, "B", "count", 0))
ROUTED_AT = STEPS + 2
SEND_STEPS = [(b, s) for b in range(ROUTE + 1, B) for s in range(STEPS)
              if (b, s) > (ROUTE + 1, 2) and not (ROUTE + 1, 10) <= (b, s) <= (ROUTE + 2, 0)]
PER_STEP = 3
EXPERTS_AT = 6


def active(b, use):
    _, _, kind, rel = use
    if kind in ("maxT", "ctxT"):
        return 0 <= GROUPS * b + rel < GROUPS * B
    if kind == "count":
        return b == ROUTE
    return 0 <= b + rel < B


FIRST_BANK = {"xnT": 7, "v0": 0, "v1": 1, "q": 2, "qrot": 3, "k": 4, "krot": 5}
SHARES = [(0, NT), (NT, 3 * NT), (TILES - LATE * NT, TILES), (3 * NT, TILES - LATE * NT)]
IDENTITY = 3
CONSTANTS = IDENTITY + 16

def place_of(h):
    return h % 2 * PAIRS + h // 2


ORDER = {}
for _b in range(-2, B + 1):
    for _u in USES:
        if active(_b, _u):
            ORDER[(_b, _u[2], _u[3])] = len(ORDER)


def at(base, slope, d):
    return base + slope * d


def block_kernel(nc, x, w_q, w_k, w_v, w_o, w_g, w1, w2, w3, cos_t, sin_t, own_head, out):
    with ExitStack() as ctx:
        def sb(name, shape, dt=F32):
            return ctx.enter_context(nc.sbuf_tensor(name, shape, dt))

        def sem(name):
            return ctx.enter_context(nc.semaphore(name))

        ps = ctx.enter_context(nc.psum_tensor("ps", [P, 8, 512], F32))
        ps_s = ps[:, 0:2, :]
        ps_m = ps[:, 2:6, :]
        ps_ctx = ps[:, 6, :]
        ps_misc = ps[:, 7, :]

        x_sb = sb("x_sb", [P, TILES, D])
        rows = sb("rows", [P, TILES, ROW])
        logits = sb("logits", [P, E, TILES])
        wqT, wkT = sb("wqT", [P, D]), sb("wkT", [P, D])
        wqr, wkr = sb("wqr", [P, D]), sb("wkr", [P, D])
        wvg = sb("wvg", [P, D + E])
        woT = sb("woT", [P, D])
        cos_sb, sin_sb = sb("cos_sb", [P, L]), sb("sin_sb", [P, L])
        ident = sb("ident", [P, P])
        ident_bf = sb("ident_bf", [P, P], BF16)
        w1_sb = sb("w1_sb", [P, E, HID])
        w3_sb = sb("w3_sb", [P, E, HID])
        w2_sb = sb("w2_sb", [P, E, CHUNKS, D])
        stats = sb("stats", [P, TILES, 6])
        mv = sb("mv", [P, TILES, 2])
        var, root, rstd = sb("var", [P, TILES]), sb("root", [P, TILES]), sb("rstd", [P, TILES])
        xn = sb("xn", [P, NT, D])
        xnT = sb("xnT", [P, L])
        v_stage = sb("v_stage", [P, NT, D])
        v_st = [sb(f"v_st{i}", [P, NT, H, 32]) for i in range(2)]
        rope_a, rope_b = sb("rope_a", [P, 2, L]), sb("rope_b", [P, 2, L])
        rest = sb("rest", [P, 2, L])
        parts = sb("parts", [P, 2, 3, L], BF16)
        q_st = [sb(f"q_st{i}", [P, PAIRS, L], BF16) for i in range(2)]
        k_st = [sb(f"k_st{i}", [P, H, L], BF16) for i in range(2)]
        negm = sb("negm", [P, 2, NT, G])
        mrest = sb("mrest", [P, NT, G])
        msplit = sb("msplit", [P, NT, G, 3], BF16)
        mrow = sb("mrow", [G * 3, L], BF16)
        probs = sb("probs", [P, 8, L])
        ctx_sb = sb("ctx_sb", [P, L])
        ctx_r = sb("ctx_r", [P, NT, G])
        ctxn = sb("ctxn", [P, NT, D])
        ctxnT = sb("ctxnT", [P, L])
        r_e, r_s, r_eq = sb("r_e", [P, E, TILES]), sb("r_s", [P, E, TILES]), sb("r_eq", [P, E, TILES])
        r_first, r_second = sb("r_first", [P, E, TILES]), sb("r_second", [P, E, TILES])
        r_top = sb("r_top", [P, 2, TILES])
        r_at = sb("r_at", [P, TILES])
        r_sum = sb("r_sum", [P, TILES])
        r_w = sb("r_w", [P, 2, TILES])
        r_mask = sb("r_mask", [P, E, TILES], BF16)
        r_cum = sb("r_cum", [P, E, TILES])
        r_zero = sb("r_zero", [P, E * TILES])
        cum_e = sb("cum_e", [P, E + 1])
        n_e, tl_e, tinc_e, off_e = (sb(n, [P, E]) for n in ("n_e", "tl_e", "tinc_e", "off_e"))
        r_cmp = sb("r_cmp", [P, E, TILES])
        ex_cmp = sb("ex_cmp", [1, XT, E - 1])
        ex_f = sb("ex_f", [1, XT])
        ex_i = sb("ex_i", [1, XT], I32)
        slot_f, slot = sb("slot_f", [P, 2, TILES]), sb("slot", [P, 2, TILES], I32)
        io_i = sb("io_i", [P, XT], I32)
        io_e = sb("io_e", [P, E])
        io_n = sb("io_n", [P, TILES])
        io_x = sb("io_x", [P, XT])
        dest = sb("dest", [P, TILES], I32)
        before = sb("before", [P, P], BF16)
        ones_bf = sb("ones_bf", [P, P], BF16)
        blank = sb("blank", [P, BLANKS, ROW])
        xt = [sb(f"xt{i}", [P, ROW]) for i in range(4)]
        xT = [xn[:, i, :] for i in range(4)]
        gate = [rest[:].rearrange("p k l -> p (k l)")[:, HID * i:HID * (i + 1)] for i in range(2)]
        flat = parts[:].rearrange("p k t l -> p (k t l)").bitcast(F32)
        hid = [flat[:, HID * i:HID * (i + 1)] for i in range(2)]
        hidT = [flat[:, 2 * HID + CHUNKS * P * i:2 * HID + CHUNKS * P * (i + 1)].rearrange("p (c n) -> p c n", n=P)
                for i in range(2)]
        y_sb = [v_stage[:, i, :] for i in range(4)]
        y_to = [sb(f"y_to{i}", [P, 1], I32) for i in range(UNROLL)]
        as_tiles = "p k (t d) -> p (k t) d"
        y_first = k_st[0][:].bitcast(F32).rearrange(as_tiles, d=D)
        y_second = [q_st[0][:].bitcast(F32).rearrange(as_tiles, d=D)[:, i:i + 2 * NT] for i in (0, 2 * NT)] + [
            a[:].rearrange(as_tiles, d=D) for a in (rope_a, rope_b)]

        slots = nc.dram_tensor("slots", (SLOT_TILES * P, ROW), F32).ap()
        results = nc.dram_tensor("results", ((2 * TILES + BLANKS) * P, D), F32).ap()

        terms = nc.dram_tensor("terms", (2, 2, TERMS, HD * H, L), BF16).ap()

        x_first, x_second, x_rest = sem("x_first"), sem("x_second"), sem("x_rest")
        w_loaded, ffn_w_loaded = sem("w_loaded"), sem("ffn_w_loaded")
        consts = sem("consts")
        zeros_made, own_loaded = sem("zeros_made"), sem("own_loaded")
        rot_made = sem("rot_made")
        scores_made, probs_made = sem("scores_made"), sem("probs_made")
        pv_done, ctx_copied = sem("pv_done"), sem("ctx_copied")
        max_scores, max_found = sem("max_scores"), sem("max_found")
        max_split, max_rows = sem("max_split"), sem("max_rows")
        misc_filled, misc_emptied = sem("misc_filled"), sem("misc_emptied")
        xn_made, v_placed, q_split, k_split = sem("xn_made"), sem("v_placed"), sem("q_split"), sem("k_split")
        q_written, k_written, stacks_loaded = sem("q_written"), sem("k_written"), sem("stacks_loaded")
        rows_kept = sem("rows_kept")
        late_made, late_turned, late_copied, late_logits, logits_kept = (
            sem("late_made"), sem("late_turned"), sem("late_copied"), sem("late_logits"), sem("logits_kept"))
        dve_seq, pool_seq, stat_seq, r_seq = sem("dve_seq"), sem("pool_seq"), sem("stat_seq"), sem("r_seq")
        var_made, root_made = sem("var_made"), sem("root_made")
        slots_blank = sem("slots_blank")
        r_shift, r_exp, r_chosen = sem("r_shift"), sem("r_exp"), sem("r_chosen")
        slots_known, experts_known = sem("slots_known"), sem("experts_known")
        first_sent, second_sent, dest_moved = sem("first_sent"), sem("second_sent"), sem("dest_moved")
        xt_loaded = [sem(f"xt_loaded{i}") for i in range(4)]
        y_sent = [sem(f"y_sent{i}") for i in range(4)]
        xT_made, xT_copied = sem("xT_made"), sem("xT_copied")
        gate_done, up_done = sem("gate_done"), sem("up_done")
        gate_made, hid_made = sem("gate_made"), sem("hid_made")
        hT_made, hidT_copied, y_made, y_copied = sem("hT_made"), sem("hidT_copied"), sem("y_made"), sem("y_copied")
        y_loaded = [sem(f"y_loaded{i}") for i in range(B // 2)]
        weights_known, combined, pool_combined, pool_sums = (
            sem("weights_known"), sem("combined"), sem("pool_combined"), sem("pool_sums"))
        stored = sem("stored")

        block = ctx.enter_context(nc.Block())
        x_dram = x.rearrange("b (t p) d -> b p t d", p=P)
        out_dram = out.rearrange("b (t p) d -> b p t d", p=P)

        def wait(eng, semaphore, value):
            if not isinstance(value, int):
                value = eng.to_reg(value)
                eng.wait_ge(x_first, 16)
            eng.wait_ge(semaphore, value)

        def use_no(b, kind, rel, d):
            return at(ORDER[(b, kind, rel)], PER_BATCH, d)

        def bank(b, kind):
            return ps[:, FIRST_BANK[kind] if b < 0 and kind in FIRST_BANK else 7, :]

        def wide(b, s):
            return b == B - 1 and s >= 2 * NT

        def score_bank(b, s, j):
            return ps[:, j if wide(b, s) else j % 2, :]

        def uses(b, s, slot):
            if b == -1:
                when = [(7, "A") if u[2] in FIRST_BANK else u[:2] for u in USES]
            else:
                when = [u[:2] for u in USES]
            return [u for u, w in zip(USES, when) if w == (s, slot) and active(b, u)]

        def pipeline(eng, step, experts):
            for b in (-2, -1):
                for s in range(STEPS):
                    step(b, s, 0)
            for s in range(5):
                step(0, s, 0)
            with eng.Fori(0, LOOPED // 2) as it:
                for u in (0, 1):
                    for s in range(5, STEPS):
                        step(u, s, it * 2)
                    for s in range(5):
                        step(u + 1, s, it * 2)
            for b in range(LOOPED, B):
                for s in range(5 if b == LOOPED else 0, STEPS):
                    step(b, s, 0)
                    if (b, s) == (B - 1, EXPERTS_AT):
                        experts()
            for s in range(5):
                step(B, s, 0)

        def expert_loop(eng, tile):
            for j in range(UNROLL):
                tile(j, 0)
            with eng.Fori(1, XT // UNROLL) as it:
                for j in range(UNROLL):
                    tile(j, it * UNROLL)
            for j in range(XT // UNROLL * UNROLL, XT):
                tile(j, 0)

        def result(c, k):
            t = NT * c
            return y_first[:, t:t + NT] if k == 0 else y_second[c // 2][:, t % (2 * NT):t % (2 * NT) + NT]

        def peeled(j, d, n):
            return isinstance(d, int) and j < n

        @block.sync
        def _(sp):
            sp.dma_start(x_sb[:, 0:NT, :], x_dram[0]).then_inc(x_first, 16)
            for src, dst in ((w_v, wvg[:, 0:D]), (w_g, wvg[:, D:D + E]), (w_q, wqT[:]), (w_k, wkT[:]),
                             (cos_t, cos_sb[:]), (sin_t, sin_sb[:]), (w_o, woT[:])):
                sp.dma_start(dst, src).then_inc(w_loaded, 16)
            for b in range(1, B):
                sp.dma_start(x_sb[:, NT * b:NT * (b + 1), :], x_dram[b]).then_inc(x_second if b < 3 else x_rest, 16)
            for i in (0, 1):
                sp.dma_start(k_st[i][ROWS:ROWS + MROWS].bitcast(F32), own_head).then_inc(own_loaded, 16)

            def write_parts(b, d):
                if b >= 1:
                    wait(sp, stacks_loaded, at(4 * 16 * b, 64, d))
                for qk in (0, 1):
                    wait(sp, (q_split, k_split)[qk], at(b + 1, 1, d))
                    for t, n, part in RUNS:
                        src = parts[:, 0, 0:n, :] if qk == 0 else parts[:, 1, part:part + 1, :].to_broadcast([P, n, L])
                        sp.dma_start(terms[b % 2, qk, t:t + n].rearrange("t r l -> r t l"), src).then_inc(
                            (q_written, k_written)[qk], 16)

            def load_stacks(b, d):
                if b >= 2:
                    wait(sp, scores_made, at(4 * STEPS * (b - 1), 4 * STEPS, d))
                for qk in (0, 1):
                    wait(sp, (q_written, k_written)[qk], at(len(RUNS) * 16 * (b + 1), len(RUNS) * 16, d))
                    for hh in (0, 1):
                        rows_ = slice(hh * TERMS * HD, (hh + 1) * TERMS * HD)
                        dst = q_st[b % 2][rows_] if qk == 0 else k_st[b % 2][rows_, hh * PAIRS:(hh + 1) * PAIRS]
                        sp.dma_start(dst.rearrange("r p l -> r (p l)"), terms[b % 2, qk].rearrange(
                            "t (two d p) l -> two t d (p l)", two=2, d=HD)[hh]).then_inc(stacks_loaded, 16)

            def step(b, s, d):
                if s == 0 and -1 <= b < B - 1 and b != 0:
                    write_parts(b + 1, d)
                if s == 2 and -1 <= b < B - 1 and b != 0:
                    if b == -1:
                        sp.wait_ge(zeros_made, 2)
                    load_stacks(b + 1, d)
                if (b, s) == (-1, 4):
                    write_parts(1, 0)
                    load_stacks(1, 0)
                if s == 7 and 0 <= b + 1 < E:
                    load_expert(b + 1, d)
                if s == 6 and 0 <= b < 4:
                    wait(sp, consts, CONSTANTS)
                    quarter = SLOT_TILES // 4
                    for i in range(0, quarter, BLANKS):
                        first = at((quarter * b + i) * P, quarter * P, d)
                        sp.dma_start(slots[bass.ds(first, BLANKS * P)].rearrange("(t p) n -> p t n", p=P),
                                     blank[:]).then_inc(slots_blank, 16)
                for u in USES:
                    if u[0] == s and u[2] == "maxT" and active(b, u):
                        grp, n = GROUPS * b + u[3], use_no(b, "maxT", u[3], d)
                        wait(sp, misc_emptied, n + 1)
                        pb = (b + u[3] // GROUPS) % 2
                        for pr in range(G // 2):
                            sp.dma_start(q_st[pb][ROWS:ROWS + MROWS, 2 * (u[3] % GROUPS) + pr, :],
                                         mrow[MROWS * pr:MROWS * (pr + 1), :]).then_inc(max_rows, 16)

                if (b, s) == (B - 1, EXPERTS_AT + 1):
                    load_results(range(0, B // 4))
                if (b, s) == (B - 1, max(EXPERTS_AT + 1, 10)):
                    load_results(range(B // 4, B // 2))
                    store_batches()

            def load_expert(e, d):
                ex = bass.ds(at(e, 1, d), 1)
                sp.dma_start(w1_sb[:, ex, :], w1[:, ex, :]).then_inc(ffn_w_loaded, 16)
                sp.dma_start(w3_sb[:, ex, :], w3[:, ex, :]).then_inc(ffn_w_loaded, 16)
                for c in range(CHUNKS):
                    n = P if c < CHUNKS - 1 else LAST
                    sp.dma_start(w2_sb[0:n, ex, c, :], w2[c * P:c * P + n, ex, :]).then_inc(ffn_w_loaded, 16)

            def load_results(pairs):
                for i in range(4):
                    sp.wait_ge(y_sent[i], 16 * len(range(i, XT, 4)))
                sp.wait_ge(scores_made, 4 * STEPS * (B - 1))
                n = 2 * NT
                for i in pairs:
                    for k, dst in ((0, y_first[:, n * i:n * (i + 1)]), (1, y_second[i])):
                        src = results[(k * TILES + n * i) * P:(k * TILES + n * (i + 1)) * P]
                        sp.dma_start(dst, src.rearrange("(t p) d -> p t d", p=P)).then_inc(y_loaded[i], 16)

            def store_batches():
                for c in range(B - 1):
                    if c in POOL_COMBINES:
                        sp.wait_ge(pool_combined, POOL_COMBINES.index(c) + 1)
                    else:
                        sp.wait_ge(combined, DVE_COMBINES.index(c) + 1)
                    sp.dma_start(out_dram[c], x_sb[:, NT * c:NT * (c + 1), :]).then_inc(stored, 16)

            def experts():
                wait(sp, second_sent, 16 * TILES)

                def tile(j, d):
                    if not peeled(j, d, 4):
                        wait(sp, xT_copied, d + (j - 3))
                    sp.dma_start(xt[j % 4][:], slots[bass.ds((d + j) * P, P), :]).then_inc(
                        xt_loaded[j % 4], 16)

                expert_loop(sp, tile)

            pipeline(sp, step, experts)
            wait(sp, misc_emptied, len(ORDER))
            c = B - 1
            sp.dma_start(out_dram[c], x_sb[:, NT * c:NT * (c + 1), :]).then_inc(stored, 16)
            sp.wait_ge(stored, 16 * B)

        @block.tensor
        def _(pe):
            pe.wait_ge(w_loaded, 7 * 16)
            pe.wait_ge(consts, IDENTITY)

            def shared(b, u, d):
                kind, rel = u[2], u[3]
                n = use_no(b, kind, rel, d)
                misc = bank(b, kind)
                if kind == "qrot" and b == -2:
                    pe.wait_ge(rot_made, 1)
                if b < 0 and kind in FIRST_BANK and kind != "xnT":
                    pe.wait_ge(misc_emptied, ORDER[(b, "xnT", 2)] + 1)
                elif ORDER[(b, kind, rel)] > 0:
                    pe.wait_ge(misc_emptied, n)
                if kind == "maxT":
                    pe.wait_ge(max_split, at(GROUPS * b + rel + 1, GROUPS, d))
                    dst = misc.bitcast(BF16)
                    for qb in range(NT):
                        last = nc.tensor.transpose(dst[0:3 * G, qb * P:(qb + 1) * P],
                                                   msplit[:, qb].rearrange("p g t -> p (g t)"), ident_bf[:])
                elif kind == "ctxT":
                    pe.wait_ge(ctx_copied, at(GROUPS * b + rel + 1, GROUPS, d))
                    for qb in range(NT):
                        last = nc.tensor.transpose(misc[:, qb * P:(qb + 1) * P],
                                                   ctx_sb[:, qb * P:(qb + 1) * P], ident[:])
                elif kind == "ctxnT":
                    for qb in range(NT):
                        last = nc.tensor.transpose(misc[:, qb * P:(qb + 1) * P], ctxn[:, qb, :], ident[:])
                elif kind == "out":
                    for qb in range(NT):
                        last = nc.tensor.matmul(misc[:, qb * P:(qb + 1) * P], ctxnT[:, qb * P:(qb + 1) * P],
                                                woT[:], start=True, stop=True)
                elif kind == "xnT":
                    if b + rel < B - LATE:
                        pe.wait_ge(xn_made, at(b + rel + 1, 1, d))
                    for t in range(NT):
                        row = xn[:, t, :] if b + rel < B - LATE else rows[:, NT * (b + rel) + t, 0:D]
                        last = nc.tensor.transpose(misc[:, t * P:(t + 1) * P], row, ident[:])
                elif kind == "count":
                    pe.wait_ge(r_chosen, 1)
                    m = r_mask[:].rearrange("p e t -> p (e t)")
                    nc.tensor.matmul(misc[:, 0:E * TILES], before[:], m, start=True, stop=True)
                    last = nc.tensor.matmul(misc[:, E * TILES:2 * E * TILES], ones_bf[:], m, start=True, stop=True)
                elif kind in ("v0", "v1"):
                    t0 = 2 * int(kind[1])
                    for t in (0, 1):
                        last = nc.tensor.matmul(misc[:, t * (D + E):(t + 1) * (D + E)],
                                                xnT[:, (t0 + t) * P:(t0 + t + 1) * P], wvg[:], start=True, stop=True)
                else:
                    w = {"q": wqT, "qrot": wqr, "k": wkT, "krot": wkr}[kind]
                    last = nc.tensor.matmul(misc[:], w[:], xnT[:], start=True, stop=True)
                last.then_inc(misc_filled, 1)

            def late_rows():
                pe.wait_ge(late_made, 1)
                for t in range(LATE * NT):
                    last = nc.tensor.transpose(ps_s[:, t // NT, t % NT * P:(t % NT + 1) * P],
                                               rows[:, NT * (B - LATE) + t, 0:D], ident[:])
                last.then_inc(late_turned, 1)

            def late_router():
                pe.wait_ge(late_copied, 1)
                for t in range(LATE * NT):
                    last = nc.tensor.matmul(ps_s[:, 0, t * E:(t + 1) * E],
                                            probs[:, t // NT, t % NT * P:(t % NT + 1) * P], wvg[:, D:D + E],
                                            start=True, stop=True)
                last.then_inc(late_logits, 1)

            def step(b, s, d):
                g, kb = s // NT, s % NT
                par, live = b % 2, 0 <= b < B
                grp = GROUPS * b + g + 2
                find = 0 <= grp < GROUPS * B
                mb, mg = (b + (g + 2) // GROUPS) % 2, (g + 2) % GROUPS
                if (b, s) == (0, 0):
                    pe.wait_ge(own_loaded, 2 * 16)
                    pe.wait_ge(logits_kept, 1)
                if live and kb == 0:
                    pe.wait_ge(max_rows, at(32 * (GROUPS * b + g + 1), 32 * GROUPS, d))
                if find and s % (2 * NT) == 0 and mg == 0:
                    pe.wait_ge(stacks_loaded, at(64 * (grp // GROUPS + 1), 64, d))
                if (b, s) == (-1, 8):
                    pe.wait_ge(misc_emptied, ORDER[(b, "krot", 2)] + 1)
                    late_rows()

                def score(j):
                    n = 4 * (STEPS * b + s) + j
                    if not live:
                        return
                    if wide(b, s) and not wide(b, s - 1) and j >= 2:
                        pe.wait_ge(max_found, 2 * STEPS * B)
                    elif wide(b, s - 1):
                        pe.wait_ge(probs_made, n - 3)
                    elif n >= 2:
                        pe.wait_ge(probs_made, at(n - 1, 4 * STEPS, d))
                    h = G * g + j
                    nc.tensor.matmul(score_bank(b, s, j), k_st[par][0:ROWS + MROWS, place_of(h), kb * P:(kb + 1) * P],
                                     q_st[par][0:ROWS + MROWS, h // 2, :],
                                     start=True, stop=True).then_inc(scores_made, 1)

                def maxima(half):
                    if not find:
                        return
                    h = G * mg + kb
                    m = 2 * (NT * grp + kb) + half
                    if m >= 2:
                        pe.wait_ge(max_found, at(m - 1, 2 * STEPS, d))
                    for qb in (2 * half, 2 * half + 1):
                        last = nc.tensor.matmul(ps_m[:, qb, :], q_st[mb][0:ROWS, h // 2, qb * P:(qb + 1) * P],
                                                k_st[mb][0:ROWS, place_of(h), :], start=True, stop=True)
                    last.then_inc(max_scores, 1)

                score(0)
                maxima(0)
                score(1)
                for u in uses(b, s, "A"):
                    shared(b, u, d)
                score(2)
                maxima(1)
                score(3)
                if (b, s) == (-1, 11):
                    late_router()
                n = STEPS * b + s - 1
                if 0 <= n < STEPS * B:
                    pb, ps_ = (b if s else b - 1) % 2, (s - 1) % STEPS
                    pg, pk = ps_ // NT, ps_ % NT
                    pe.wait_ge(probs_made, at(4 * (n + 1), 4 * STEPS, d))
                    if pk == 0 and n >= NT:
                        pe.wait_ge(ctx_copied, at(n // NT, GROUPS, d))
                    if pk == 0 and pg == 0:
                        pe.wait_ge(v_placed, at(n // STEPS + 1, 1, d))
                    for j in range(G):
                        last = nc.tensor.matmul(ps_ctx[32 * j:32 * j + 32, :], v_st[pb][:, pk, G * pg + j, :],
                                                probs[:, 4 * (ps_ % 2) + j, :], start=(pk == 0), stop=(pk == NT - 1))
                    last.then_inc(pv_done, 1)
                for u in uses(b, s, "B"):
                    shared(b, u, d)

            def experts():
                pe.wait_ge(ffn_w_loaded, (2 + CHUNKS) * E * 16)
                pe.wait_ge(experts_known, 1)
                pe.wait_ge(misc_emptied, 1 + max(ORDER[(B - 1,) + u[2:]] for u in USES
                                                 if active(B - 1, u) and u[0] <= EXPERTS_AT))
                pe.wait_ge(probs_made, 4 * (STEPS * (B - 1) + EXPERTS_AT + 1))
                pe.wait_ge(max_found, 2 * min(STEPS * B, STEPS * (B - 1) + EXPERTS_AT + 1 + 2 * NT))

                expert = [pe.alloc_register(f"expert{i}") for i in range(4)]

                def load_expert(j, d):
                    pe.reg_load(expert[j % 4], ex_i[0:1, bass.ds(d + j, 1)])

                def expert_of(j):
                    return pe.snap(expert[j % 4], min_val=0, max_val=E - 1)

                def turn(j, d):
                    pe.wait_ge(xt_loaded[j % 4], at(16 * (j // 4 + 1), 4, d))
                    if not peeled(j, d, 1):
                        pe.wait_ge(xT_copied, d + j)
                    nc.tensor.transpose(ps[:, 7, 0:P], xt[j % 4][:, 0:D], ident[:]).then_inc(xT_made, 1)

                def up(j, e, k):
                    nc.tensor.matmul(ps[:, 2 * (j % 2) + k, 0:HID], xT[j % 4],
                                     (w1_sb, w3_sb)[k][:, bass.ds(e, 1), :].rearrange("p a n -> p (a n)"),
                                     start=True, stop=True).then_inc((gate_done, up_done)[k], 1)

                def turn_hidden(j, d):
                    pe.wait_ge(hid_made, d + (j + 1))
                    if not peeled(j, d, 1):
                        pe.wait_ge(hidT_copied, d + j)
                    for c in range(CHUNKS):
                        m = P if c < CHUNKS - 1 else LAST
                        last = nc.tensor.transpose(ps[0:m, 4, c * P:(c + 1) * P], hid[j % 2][:, c * P:c * P + m],
                                                   ident[:])
                    last.then_inc(hT_made, 1)

                def down(j, d):
                    e = expert_of(j)
                    pe.wait_ge(hidT_copied, d + (j + 1))
                    if not peeled(j, d, 1):
                        pe.wait_ge(y_copied, d + j)
                    for c in range(CHUNKS):
                        m = P if c < CHUNKS - 1 else LAST
                        last = nc.tensor.matmul(ps[:, 5, 0:D], hidT[j % 2][0:m, c, :],
                                                w2_sb[0:m, bass.ds(e, 1), c, :].rearrange("p a n -> p (a n)"),
                                                start=(c == 0), stop=(c == CHUNKS - 1))
                    last.then_inc(y_made, 1)

                def tile(j, d):
                    e = expert_of(j)
                    pe.wait_ge(xT_copied, d + (j + 1))
                    if not peeled(j, d, 2):
                        pe.wait_ge(hid_made, d + (j - 1))
                    up(j, e, 0)
                    up(j, e, 1)
                    if not (isinstance(d, int) and j == XT - 1):
                        load_expert(j + 1, d)
                    if not peeled(j, d, 2):
                        down(j - 2, d)
                    if not (isinstance(d, int) and j >= XT - 2):
                        turn(j + 2, d)
                    if not peeled(j, d, 1):
                        turn_hidden(j - 1, d)

                load_expert(0, 0)
                turn(0, 0)
                turn(1, 0)
                expert_loop(pe, tile)
                down(XT - 2, 0)
                turn_hidden(XT - 1, 0)
                down(XT - 1, 0)
                pe.wait_ge(y_copied, XT)

            pipeline(pe, step, experts)

        @block.scalar
        def _(act):
            def shared(b, u, d):
                kind, rel = u[2], u[3]
                if kind not in ("maxT", "ctxnT", "xnT", "v0", "v1"):
                    return
                n = use_no(b, kind, rel, d)
                misc = bank(b, kind)
                act.wait_ge(misc_filled, n + 1)
                if kind == "maxT":
                    if GROUPS * b + rel >= 1:
                        act.wait_ge(max_rows, at(32 * (GROUPS * b + rel), 32 * GROUPS, d))
                    nc.scalar.copy(mrow[:], misc.bitcast(BF16)[0:3 * G, 0:L]).then_inc(misc_emptied, 1)
                elif kind == "ctxnT":
                    nc.scalar.copy(ctxnT[:], misc[:]).then_inc(misc_emptied, 1)
                elif kind == "xnT":
                    nc.scalar.copy(xnT[:], misc[:]).then_inc(misc_emptied, 1)
                else:
                    t0 = 2 * int(kind[1])
                    if kind == "v0" and b + rel >= 1:
                        act.wait_ge(v_placed, at(b + rel, 1, d))
                    both = misc[:, 0:2 * (D + E)].rearrange("p (t n) -> p t n", t=2)
                    last = nc.scalar.copy(v_stage[:, t0:t0 + 2, :], both[:, :, 0:D])
                    if b + rel < B - LATE:
                        last = nc.scalar.copy(logits[:, :, bass.ds(at(NT * (b + rel) + t0, NT, d), 2)],
                                              both[:, :, D:D + E].rearrange("p t e -> p e t"))
                    last.then_inc(misc_emptied, 1)

            def step(b, s, d):
                live = 0 <= b < B
                if (b, s) == (-2, 0):
                    deviations(0)

                def exps(j0, j1):
                    for j in range(j0, j1):
                        n = 4 * (STEPS * b + s) + j
                        if j % 4 == 0 and n >= 8:
                            act.wait_ge(pv_done, at(n // 4 - 1, STEPS, d))
                        act.wait_ge(scores_made, at(n + 1, 4 * STEPS, d))
                        nc.scalar.activation(probs[:, n % 8, :], score_bank(b, s, j), ACT.Exp,
                                             scale=float(HD) ** -0.5).then_inc(probs_made, 1)

                if live:
                    exps(0, 1)
                for u in uses(b, s - 1, "B"):
                    shared(b, u, d)
                n = STEPS * b + s - 1
                if n >= NT and n % NT == 0 and n // NT <= GROUPS * B:
                    copy_context(n // NT - 1, b, d)
                if live:
                    exps(1, 4)
                for u in uses(b, s, "A"):
                    shared(b, u, d)
                if (b, s) == (-2, 7):
                    deviations(1)
                if (b, s) == (-1, 7):
                    deviations(2)
                    deviations(3)
                if (b, s) == (-1, 8):
                    act.wait_ge(late_turned, 1)
                    nc.scalar.copy(probs[:, 0:LATE, :], ps_s[:, 0:LATE, :]).then_inc(late_copied, 1)
                if (b, s) == (-1, 11):
                    act.wait_ge(late_logits, 1)
                    nc.scalar.copy(logits[:, :, NT * (B - LATE):], ps_s[:, 0, 0:LATE * NT * E].rearrange(
                        "p (t e) -> p e t", e=E)).then_inc(logits_kept, 1)
                if (b, s) == (ROUTE, 6):
                    act.wait_ge(r_shift, 1)
                    nc.scalar.activation(r_e[:], r_s[:], ACT.Exp).then_inc(r_exp, 1)

            def deviations(no):
                t0, t1 = SHARES[no]
                act.wait_ge(var_made, no + 1)
                nc.scalar.activation(root[:, t0:t1], var[:, t0:t1], ACT.Sqrt).then_inc(root_made, 1)

            def copy_context(grp, b, d):
                act.wait_ge(pv_done, at(NT * (grp + 1), STEPS, d))
                if grp >= 1:
                    act.wait_ge(misc_filled, ctx_use(grp - 1, b, d) + 1)
                nc.scalar.copy(ctx_sb[:], ps_ctx[:]).then_inc(ctx_copied, 1)

            def ctx_use(grp, b, d):
                for (bb, kind, rel), n in ORDER.items():
                    if kind == "ctxT" and GROUPS * bb + rel == grp:
                        return at(n, PER_BATCH, d)

            def experts():
                def tile(j, d):
                    act.wait_ge(gate_done, d + (j + 1))
                    if not peeled(j, d, 2):
                        act.wait_ge(hid_made, d + (j - 1))
                    nc.scalar.activation(gate[j % 2], ps[:, 2 * (j % 2), 0:HID], ACT.Silu).then_inc(gate_made, 1)
                    if not peeled(j, d, 1):
                        back(j - 1, d)

                def back(j, d):
                    act.wait_ge(hT_made, d + (j + 1))
                    if not peeled(j, d, 2):
                        act.wait_ge(y_made, d + (j - 1))
                    nc.scalar.copy(hidT[j % 2][:, 0:CHUNKS - 1, :],
                                   ps[:, 4, 0:(CHUNKS - 1) * P].rearrange("p (c n) -> p c n", n=P))
                    nc.scalar.copy(hidT[j % 2][0:LAST, CHUNKS - 1, :],
                                   ps[0:LAST, 4, (CHUNKS - 1) * P:CHUNKS * P]).then_inc(hidT_copied, 1)

                expert_loop(act, tile)
                back(XT - 1, 0)

            pipeline(act, step, experts)

        @block.vector
        def _(dve):
            def link(ins):
                ins.then_inc(dve_seq, 1)
                return ins

            nc.vector.memset(k_st[0][0:ROWS].bitcast(F32), 0.0).then_inc(zeros_made, 1)
            seq_at, tot = {}, 4 * len(SHARES)
            for bb in range(-2, B + 1):
                for u in USES:
                    if u[2] == "ctxT" and active(bb, u):
                        seq_at[("ctx", bb, u[3])] = tot
                        tot += 1
            PER = GROUPS

            def statistics(no):
                t0, t1 = SHARES[no]
                base = 4 * no
                for t in range(t0, t1):
                    last = nc.vector.bn_stats(stats[:, t, :], x_sb[:, t, :])
                link(last)
                dve.wait_ge(dve_seq, base + 1)
                for t in range(t0, t1):
                    last = nc.vector.bn_aggr(mv[:, t, :], stats[:, t, :])
                link(last)
                dve.wait_ge(dve_seq, base + 2)
                nc.vector.tensor_scalar(var[:, t0:t1], mv[:, t0:t1, 1], EPS, None, ALU.add).then_inc(var_made, 1)
                dve.wait_ge(root_made, no + 1)
                nc.vector.reciprocal(rstd[:, t0:t1], root[:, t0:t1]).then_inc(stat_seq, 1)
                dve.wait_ge(stat_seq, 3 * no + 1)
                link(nc.vector.tensor_tensor(rstd[:, t0:t1], var[:, t0:t1], rstd[:, t0:t1], ALU.mult))
                dve.wait_ge(dve_seq, base + 3)
                link(nc.vector.tensor_tensor(root[:, t0:t1], rstd[:, t0:t1], root[:, t0:t1], ALU.add))
                dve.wait_ge(dve_seq, base + 4)
                nc.vector.tensor_scalar(root[:, t0:t1], root[:, t0:t1], 0.5, None, ALU.mult).then_inc(stat_seq, 1)
                dve.wait_ge(stat_seq, 3 * no + 2)
                nc.vector.reciprocal(rstd[:, t0:t1], root[:, t0:t1]).then_inc(stat_seq, 1)
                dve.wait_ge(stat_seq, 3 * no + 3)

            def rotated_weights():
                dve.wait_ge(w_loaded, 7 * 16)
                for src, dst in ((wqT, wqr), (wkT, wkr)):
                    s2, d2 = (a[:].rearrange("p (n two h) -> p n two h", two=2, h=PAIRS) for a in (src, dst))
                    nc.vector.tensor_scalar(d2[:, :, 0, :], s2[:, :, 1, :], -1.0, None, ALU.mult)
                    last = nc.vector.tensor_copy(d2[:, :, 1, :], s2[:, :, 0, :])
                last.then_inc(rot_made, 1)

            def layer_norm(b, d):
                if b == -2:
                    dve.wait_ge(x_first, 16)
                    statistics(0)
                if b == -1:
                    dve.wait_ge(x_second, 16 * 2)
                    statistics(1)
                if b + 2 >= 1:
                    dve.wait_ge(misc_filled, use_no(b - 1, "xnT", 2, d) + 1)
                    dve.wait_ge(rows_kept, at(b + 2, 1, d))
                for t in range(NT):
                    nt = bass.ds(at(NT * (b + 2) + t, NT, d), 1)
                    last = nc.vector.tensor_scalar(xn[:, t, :], x_sb[:, nt, :].rearrange("p a n -> p (a n)"),
                                                   mv[:, nt, 0], rstd[:, nt], ALU.subtract, ALU.mult)
                last.then_inc(xn_made, 1)
                if b == -2:
                    rotated_weights()

            def split(qk):
                a, rs = rope_a[:, qk, :], rest[:, qk, :]
                then(nc.vector.tensor_tensor(a, a, rope_b[:, qk, :], ALU.add))
                then(nc.vector.tensor_copy(parts[:, qk, 0, :], a))
                then(nc.vector.tensor_tensor(rs, a, parts[:, qk, 0, :], ALU.subtract))
                then(nc.vector.tensor_copy(parts[:, qk, 1, :], rs))
                nc.vector.tensor_tensor(parts[:, qk, 2, :], rs, parts[:, qk, 1, :], ALU.subtract).then_inc(
                    (q_split, k_split)[qk], 1)

            def shared(b, u, d):
                kind, rel = u[2], u[3]
                if kind in ("maxT", "ctxnT", "xnT", "v0", "v1"):
                    return
                n = use_no(b, kind, rel, d)
                dve.wait_ge(misc_filled, n + 1)
                if kind == "ctxT":
                    g = (GROUPS + rel) % GROUPS
                    t4 = ps_misc.rearrange("p (q j c) -> p q j c", q=NT, j=G)
                    link(nc.vector.reciprocal(ctx_r[:], t4[:, :, :, HD]))
                    dve.wait_ge(dve_seq, at(seq_at[("ctx", b, rel)] + 1, PER, d))
                    nc.vector.tensor_tensor(
                        ctxn[:, :, g * G * HD:(g + 1) * G * HD].rearrange("p q (j c) -> p q j c", j=G),
                        t4[:, :, :, 0:HD], ctx_r[:].rearrange("p q (j one) -> p q j one", one=1).to_broadcast(
                            [P, NT, G, HD]), ALU.mult).then_inc(misc_emptied, 1)
                elif kind == "out":
                    sl = x_sb[:, bass.ds(at(NT * (b + rel), NT, d), NT), :]
                    if b + rel == B - 1:
                        dve.wait_ge(combined, len(DVE_COMBINES))
                    nc.vector.tensor_tensor(sl, ps_misc.rearrange("p (t n) -> p t n", t=NT), sl,
                                            ALU.add).then_inc(misc_emptied, 1)
                elif kind == "count":
                    place()
                else:
                    if kind == "q" and b + rel >= 1:
                        dve.wait_ge(k_split, at(b + rel, 1, d))
                    dst = (rope_a if kind in "qk" else rope_b)[:, 0 if kind[0] == "q" else 1, :]
                    nc.vector.tensor_tensor(dst, bank(b, kind), (cos_sb if kind in "qk" else sin_sb)[:],
                                            ALU.mult).then_inc(misc_emptied, 1)
                    if b == -2 and kind in ("qrot", "krot"):
                        dve.wait_ge(misc_emptied, ORDER[(-2, kind, 2)] + 1)
                        split(0 if kind == "qrot" else 1)

            def step(b, s, d):
                g, kb = s // NT, s % NT
                grp = GROUPS * b + g + 2

                def reduce(half):
                    m = 2 * (NT * grp + kb) + half
                    dve.wait_ge(max_scores, at(m + 1, 2 * STEPS, d))
                    nc.vector.tensor_reduce(negm[:, g % 2, 2 * half:2 * half + 2, kb],
                                            ps_m[:, 2 * half:2 * half + 2, :], axis=AX.X, op=ALU.max,
                                            negate=True).then_inc(max_found, 1)

                if 0 <= grp < GROUPS * B:
                    if kb == 0 and grp >= 2:
                        dve.wait_ge(max_split, at(grp - 1, GROUPS, d))
                    reduce(0)
                if (b, s) == (-2, 0):
                    layer_norm(-2, 0)
                if s == 14 and 0 <= b + 1 < B - LATE - 2:
                    layer_norm(b + 1, d)
                if (b, s) == (-2, 6):
                    layer_norm(-1, 0)
                if (b, s) == (-1, 6):
                    dve.wait_ge(x_rest, 16 * (B - 3))
                    statistics(2)
                    for t in range(*SHARES[2]):
                        last = nc.vector.tensor_scalar(rows[:, t, 0:D], x_sb[:, t, :], mv[:, t:t + 1, 0],
                                                       rstd[:, t:t + 1], ALU.subtract, ALU.mult)
                    last.then_inc(late_made, 1)
                for u in uses(b, s, "A"):
                    shared(b, u, d)
                if 0 <= grp < GROUPS * B:
                    reduce(1)
                if (b, s) == (-1, 7):
                    statistics(3)
                r = STEPS * (b - ROUTE) + s
                if r == 5:
                    shift_logits()
                if r == 7:
                    scores()
                if 8 <= r < 12:
                    choose((r - 8) // 2, (r - 8) % 2)
                for u in uses(b, s, "B"):
                    shared(b, u, d)
                if ROUTED_AT - 4 < r <= ROUTED_AT:
                    find_slots(r - ROUTED_AT + 3)
                if r == ROUTED_AT + 4:
                    weigh()
                i = STEPS * (b - B + 1) + s - EXPERTS_AT - 2
                if 0 <= i < len(DVE_COMBINES):
                    combine(DVE_COMBINES[i])

            chain = [0]

            def then(ins):
                chain[0] += 1
                ins.then_inc(r_seq, 1)
                dve.wait_ge(r_seq, chain[0])

            def by_tile(a):
                return a.rearrange("p e t -> p t e")

            def over_e(a, n=E):
                return a.rearrange("p (one t) -> p one t", one=1).to_broadcast([P, n, TILES])

            def over_t(a):
                return a.rearrange("p (e one) -> p e one", one=1).to_broadcast([P, E, TILES])

            def shift_logits():
                dve.wait_ge(misc_emptied, ORDER[(B - LATE - 3, "v1", 2)] + 1)
                dve.wait_ge(logits_kept, 1)
                then(nc.vector.tensor_reduce(r_sum[:], by_tile(logits[:]), axis=AX.X, op=ALU.max))
                nc.vector.tensor_tensor(r_s[:], logits[:], over_e(r_sum[:]), ALU.subtract).then_inc(r_shift, 1)

            def scores():
                dve.wait_ge(r_exp, 1)
                then(nc.vector.tensor_reduce(r_sum[:], by_tile(r_e[:]), axis=AX.X, op=ALU.add))
                then(nc.vector.reciprocal(r_sum[:], r_sum[:]))
                then(nc.vector.tensor_tensor(r_s[:], r_e[:], over_e(r_sum[:]), ALU.mult))

            def choose(k, half):
                one_hot = (r_first, r_second)[k]
                if half == 0:
                    dve.wait_ge(consts, CONSTANTS)
                    then(nc.vector.tensor_reduce(r_top[:, k, :], by_tile(r_s[:]), axis=AX.X, op=ALU.max))
                    then(nc.vector.tensor_tensor(r_eq[:], r_s[:], over_e(r_top[:, k, :]), ALU.is_equal))
                    then(nc.vector.tensor_tensor(r_eq[:], r_eq[:], over_t(io_e[:]), ALU.mult))
                    return
                then(nc.vector.tensor_reduce(r_at[:], by_tile(r_eq[:]), axis=AX.X, op=ALU.min))
                then(nc.vector.tensor_tensor(one_hot[:], over_t(io_e[:]), over_e(r_at[:]), ALU.is_equal))
                if k == 0:
                    then(nc.vector.scalar_tensor_tensor(r_s[:], r_first[:], -4.0, r_s[:], op0=ALU.mult, op1=ALU.add))
                else:
                    nc.vector.tensor_tensor(r_mask[:], r_first[:], r_second[:], ALU.add).then_inc(r_chosen, 1)

            def place():
                total = ps_misc[:, E * TILES:2 * E * TILES]
                flat = r_cum[:].rearrange("p e t -> p (e t)")
                then(nc.vector.tensor_tensor_scan(flat, total, r_zero[:], 0.0, ALU.add, ALU.add))
                then(nc.vector.tensor_copy(cum_e[:, 1:E + 1], r_cum[:, :, TILES - 1]))
                then(nc.vector.tensor_tensor(flat, flat, total, ALU.subtract))
                nc.vector.tensor_tensor(flat, flat, ps_misc[:, 0:E * TILES], ALU.add).then_inc(misc_emptied, 1)

            def find_slots(share):
                if share == 0:
                    then(nc.vector.tensor_tensor(n_e[:], cum_e[:, 1:E + 1], cum_e[:, 0:E], ALU.subtract))
                    then(nc.vector.tensor_tensor(r_cmp[:], over_t(n_e[:]), over_e(io_n[:]), ALU.is_gt))
                    then(nc.vector.tensor_reduce(tl_e[:], r_cmp[:], axis=AX.X, op=ALU.add))
                    then(nc.vector.tensor_tensor_scan(tinc_e[:], tl_e[:], r_zero[:, 0:E], 0.0, ALU.add, ALU.add))
                if share == 1:
                    then(nc.vector.tensor_tensor(off_e[:], tinc_e[:], tl_e[:], ALU.subtract))
                    then(nc.vector.scalar_tensor_tensor(off_e[:], off_e[:], float(P), cum_e[:, 0:E], op0=ALU.mult,
                                                        op1=ALU.subtract))
                    dve.wait_ge(misc_emptied, ORDER[(ROUTE, "count", 0)] + 1)
                    then(nc.vector.tensor_tensor(r_cum[:], r_cum[:], over_t(off_e[:]), ALU.add))
                    then(nc.vector.tensor_tensor(r_cmp[:], r_first[:], r_cum[:], ALU.mult))
                if share == 2:
                    then(nc.vector.tensor_reduce(slot_f[:, 0, :], by_tile(r_cmp[:]), axis=AX.X, op=ALU.add))
                    then(nc.vector.tensor_tensor(r_cmp[:], r_second[:], r_cum[:], ALU.mult))
                    then(nc.vector.tensor_reduce(slot_f[:, 1, :], by_tile(r_cmp[:]), axis=AX.X, op=ALU.add))
                    nc.vector.tensor_copy(slot[:], slot_f[:]).then_inc(slots_known, 1)
                if share == 3:
                    then(nc.vector.tensor_tensor(
                        ex_cmp[:], io_x[0:1, :].rearrange("p (x one) -> p x one", one=1).to_broadcast([1, XT, E - 1]),
                        tinc_e[0:1, 0:E - 1].rearrange("p (one e) -> p one e", one=1).to_broadcast([1, XT, E - 1]),
                        ALU.is_ge))
                    then(nc.vector.tensor_reduce(ex_f[:], ex_cmp[:], axis=AX.X, op=ALU.add))
                    nc.vector.tensor_copy(ex_i[:], ex_f[:]).then_inc(experts_known, 1)

            def weigh():
                then(nc.vector.tensor_tensor(r_sum[:], r_top[:, 0, :], r_top[:, 1, :], ALU.add))
                then(nc.vector.tensor_scalar(r_sum[:], r_sum[:], 1e-20, None, ALU.add))
                then(nc.vector.reciprocal(r_sum[:], r_sum[:]))
                nc.vector.tensor_tensor(r_w[:, 0, :], r_top[:, 0, :], r_sum[:], ALU.mult).then_inc(weights_known, 1)
                nc.vector.tensor_tensor(r_w[:, 1, :], r_top[:, 1, :], r_sum[:], ALU.mult).then_inc(weights_known, 1)
                dve.wait_ge(weights_known, 2)

            def combine(c):
                dve.wait_ge(y_loaded[c // 2], 32)
                dve.wait_ge(misc_emptied, ORDER[(B - 1, "out", -1)] + 1)
                for k in (0, 1):
                    for t in range(NT):
                        x_t = x_sb[:, NT * c + t, :]
                        weight = r_w[:, k, NT * c + t:NT * c + t + 1]
                        last = nc.vector.scalar_tensor_tensor(x_t, result(c, k)[:, t], weight, x_t,
                                                              op0=ALU.mult, op1=ALU.add)
                    if k == 0:
                        then(last)
                last.then_inc(combined, 1)

            def experts():
                def copy_xT(j, d):
                    dve.wait_ge(xT_made, d + (j + 1))
                    if not peeled(j, d, UNROLL):
                        dve.wait_ge(y_sent[j % 4], at(16 * (j // 4 - 1), 4, d))
                    nc.vector.tensor_copy(y_to[j % UNROLL][:], xt[j % 4][:, D:D + 1].bitcast(I32))
                    if not peeled(j, d, 4):
                        dve.wait_ge(up_done, d + (j - 3))
                    nc.vector.tensor_copy(xT[j % 4], ps[:, 7, 0:P]).then_inc(xT_copied, 1)

                def copy_y(j, d):
                    dve.wait_ge(y_made, d + (j + 1))
                    if not peeled(j, d, 4):
                        dve.wait_ge(y_sent[j % 4], at(16 * (j // 4), 4, d))
                    nc.vector.tensor_copy(y_sb[j % 4], ps[:, 5, 0:D]).then_inc(y_copied, 1)

                def tile(j, d):
                    dve.wait_ge(gate_made, d + (j + 1))
                    dve.wait_ge(up_done, d + (j + 1))
                    if not peeled(j, d, 2):
                        dve.wait_ge(hT_made, d + (j - 1))
                    nc.vector.tensor_tensor(hid[j % 2], gate[j % 2], ps[:, 2 * (j % 2) + 1, 0:HID],
                                            ALU.mult).then_inc(hid_made, 1)
                    if not peeled(j, d, 2):
                        copy_y(j - 2, d)
                    if not (isinstance(d, int) and j >= XT - 2):
                        copy_xT(j + 2, d)

                copy_xT(0, 0)
                copy_xT(1, 0)
                expert_loop(dve, tile)
                copy_y(XT - 2, 0)
                copy_y(XT - 1, 0)

            nc.vector.memset(r_zero[:], 0.0)
            nc.vector.memset(ones_bf[:], 1.0)
            then(nc.vector.memset(cum_e[:, 0:1], 0.0))
            pipeline(dve, step, experts)

        @block.gpsimd
        def _(pool):
            made = [0]

            def then(ins):
                made[0] += 1
                ins.then_inc(consts, 1)
                pool.wait_ge(consts, made[0])

            then(nc.gpsimd.memset(ident[:], 0.0))
            then(nc.gpsimd.affine_select(out=ident[:], in_=ident[:], compare_op=ALU.not_equal, fill=1.0, base=0,
                                         pattern=[[-1, P]], channel_multiplier=1))
            then(nc.gpsimd.tensor_copy(ident_bf[:], ident[:]))
            assert made[0] == IDENTITY
            nc.gpsimd.memset(k_st[1][0:ROWS].bitcast(F32), 0.0).then_inc(zeros_made, 1)

            def more_constants():
                for i in (0, 1):
                    v = v_st[i][:].rearrange("p k h c -> p (k h) c")
                    then(nc.gpsimd.memset(v[:, :, HD:32], 0.0))
                    then(nc.gpsimd.memset(v[:, :, HD:HD + 1], 1.0))
                then(nc.gpsimd.memset(before[:], 1.0))
                then(nc.gpsimd.affine_select(out=before[:], in_=before[:], compare_op=ALU.is_gt, fill=0.0, base=0,
                                             pattern=[[1, P]], channel_multiplier=-1))
                for n, base, step_, dst in ((E, -E, 1, io_e), (TILES, 0, P, io_n), (XT, 0, 1, io_x)):
                    then(nc.gpsimd.iota(io_i[:, 0:n], pattern=[[step_, n]], base=base, channel_multiplier=0))
                    then(nc.gpsimd.tensor_copy(dst[:], io_i[:, 0:n]))
                then(nc.gpsimd.iota(dest[:], pattern=[[P, TILES]], base=0, channel_multiplier=1))
                then(nc.gpsimd.tensor_copy(rows[:, :, D].bitcast(I32), dest[:]))
                then(nc.gpsimd.memset(blank[:], 0.0))
                then(nc.gpsimd.iota(blank[:, :, D].bitcast(I32), pattern=[[P, BLANKS]], base=2 * TILES * P,
                                    channel_multiplier=1))
                assert made[0] == CONSTANTS

            M_LINKS, S_LINKS = 3, 4
            seq_at, tot = {}, 0
            for bb in range(-2, B + 1):
                for ss in range(STEPS):
                    if ss % NT == 0 and 0 <= GROUPS * bb + ss // NT + 1 < GROUPS * B:
                        seq_at[("m", bb, ss)] = tot
                        tot += M_LINKS
                    if (bb, ss) == (-1, 9) or ss == 12 and 2 <= bb + 2 < B:
                        seq_at[("s", bb)] = tot
                        tot += 2 * S_LINKS
            PER = GROUPS * M_LINKS + 2 * S_LINKS

            def link(ins, base, i, d):
                ins.then_inc(pool_seq, 1)
                wait(pool, pool_seq, at(base + i, PER, d))

            def step(b, s, d):
                g, kb = s // NT, s % NT
                grp = GROUPS * b + g + 1
                if kb == 0 and 0 <= grp < GROUPS * B:
                    base = seq_at[("m", b, s)]
                    wait(pool, max_found, at(2 * NT * (grp + 1), 2 * STEPS, d))
                    if grp >= 1:
                        bb, rel = (b, g) if g else (b - 1, GROUPS)
                        wait(pool, misc_filled, use_no(bb, "maxT", rel, d) + 1)
                    src = negm[:, (g + 1) % 2]
                    link(nc.gpsimd.tensor_copy(msplit[:, :, :, 0], src), base, 1, d)
                    link(nc.gpsimd.tensor_tensor(mrest[:], src, msplit[:, :, :, 0], ALU.subtract), base, 2, d)
                    link(nc.gpsimd.tensor_copy(msplit[:, :, :, 1], mrest[:]), base, 3, d)
                    nc.gpsimd.tensor_tensor(msplit[:, :, :, 2], mrest[:], msplit[:, :, :, 1],
                                            ALU.subtract).then_inc(max_split, 1)
                if s == 1 and 0 <= b + 1 < B:
                    wait(pool, misc_emptied, use_no(b - 1, "krot" if b <= 0 else "v1", 2, d) + 1)
                    if b >= 1:
                        wait(pool, pv_done, at(STEPS * b, STEPS, d))
                    last = None
                    for t in range(NT):
                        last = nc.gpsimd.tensor_copy(v_st[(b + 1) % 2][:, t, :, 0:HD],
                                                     v_stage[:, t, :].rearrange("p (h c) -> p h c", h=H))
                    last.then_inc(v_placed, 1)
                if s == (2 if b >= 0 else 8) and 0 <= b + 2 < B - LATE:
                    wait(pool, xn_made, at(b + 3, 1, d))
                    nc.gpsimd.tensor_copy(rows[:, bass.ds(at(NT * (b + 2), NT, d), NT), 0:D],
                                          xn[:]).then_inc(rows_kept, 1)
                if (b, s) in SEND_STEPS:
                    send(SEND_STEPS.index((b, s)))
                if s == (12 if b >= 0 else 9) and 1 <= b + 2 < B:
                    base = seq_at[("s", b)]
                    for qk, kind in ((0, "qrot"), (1, "krot")):
                        wait(pool, (q_written, k_written)[qk], at(len(RUNS) * 16 * (b + 2), len(RUNS) * 16, d))
                        wait(pool, misc_emptied, use_no(b, "krot" if b == -1 else kind, 2, d) + 1)
                        a, r = rope_a[:, qk, :], rest[:, qk, :]
                        link(nc.gpsimd.tensor_tensor(a, a, rope_b[:, qk, :], ALU.add), base, 1, d)
                        link(nc.gpsimd.tensor_copy(parts[:, qk, 0, :], a), base, 2, d)
                        link(nc.gpsimd.tensor_tensor(r, a, parts[:, qk, 0, :], ALU.subtract), base, 3, d)
                        link(nc.gpsimd.tensor_copy(parts[:, qk, 1, :], r), base, 4, d)
                        nc.gpsimd.tensor_tensor(parts[:, qk, 2, :], r, parts[:, qk, 1, :], ALU.subtract).then_inc(
                            (q_split, k_split)[qk], 1)
                        base += S_LINKS
                if (b, s) == (-2, 12):
                    more_constants()
                if (b, s) == (B - 1, max(EXPERTS_AT + 1, 9)):
                    combine_some()

            def send(i):
                for n in range(i * PER_STEP, min((i + 1) * PER_STEP, 2 * TILES)):
                    k, t = n // TILES, n % TILES
                    if n == 0:
                        pool.wait_ge(slots_known, 1)
                        pool.wait_ge(slots_blank, 16 * (SLOT_TILES // BLANKS))
                        pool.wait_ge(rows_kept, B - LATE)
                        pool.wait_ge(late_made, 1)
                    if n == TILES:
                        pool.wait_ge(first_sent, 16 * TILES)
                        nc.gpsimd.iota(rows[:, :, D].bitcast(I32), pattern=[[P, TILES]], base=TILES * P,
                                       channel_multiplier=1).then_inc(dest_moved, 1)
                        pool.wait_ge(dest_moved, 1)
                    nc.gpsimd.indirect_dma_start(
                        out=slots, out_offset=bass.IndirectOffsetOnAxis(ap=slot[:, k, t:t + 1], axis=0),
                        in_=rows[:, t, :], in_offset=None).then_inc((first_sent, second_sent)[k], 16)

            def combine_some():
                for i, c in enumerate(POOL_COMBINES):
                    pool.wait_ge(weights_known, 2)
                    pool.wait_ge(y_loaded[c // 2], 32)
                    pool.wait_ge(misc_emptied, ORDER[(B - 1, "out", -1)] + 1)
                    x_c = x_sb[:, NT * c:NT * (c + 1), :]
                    for k in (0, 1):
                        w = r_w[:, k, NT * c:NT * (c + 1)].rearrange("p (t one) -> p t one", one=1)
                        nc.gpsimd.tensor_tensor(result(c, k), result(c, k), w.to_broadcast([P, NT, D]),
                                                ALU.mult).then_inc(pool_sums, 1)
                    for k in (0, 1):
                        pool.wait_ge(pool_sums, 3 * i + 2 + k)
                        nc.gpsimd.tensor_tensor(x_c, result(c, k), x_c, ALU.add).then_inc(
                            (pool_sums, pool_combined)[k], 1)

            def experts():
                def tile(j, d):
                    wait(pool, y_copied, d + (j + 1))
                    nc.gpsimd.indirect_dma_start(
                        out=results, out_offset=bass.IndirectOffsetOnAxis(ap=y_to[j % UNROLL][:], axis=0),
                        in_=y_sb[j % 4], in_offset=None).then_inc(y_sent[j % 4], 16)

                expert_loop(pool, tile)

            pipeline(pool, step, experts)


INS = ["x", "w_q", "w_k", "w_v", "w_o", "w_g", "w1", "w2", "w3", "cos_t", "sin_t", "own_head"]


def kernel(L0_attn_x, L0_attn_W_Q, L0_attn_W_K, L0_attn_W_V, L0_attn_W_O, L0_ffn_Wg, L0_ffn_W1, L0_ffn_W2, L0_ffn_W3):
    import numpy as np
    import concourse.bacc as bacc
    from concourse.bass_utils import run_bass_kernel_spmd

    inv = np.float32(1.0) / np.float32(10000.0) ** (np.arange(0, HD, 2, dtype=np.float32) / np.float32(HD))
    angle = np.outer(inv, np.arange(L, dtype=np.float32)).astype(np.float32)
    cos_t, sin_t = (np.tile(np.repeat(f(angle), 2 * PAIRS, axis=0), (2, 1)).astype(np.float32)
                    for f in (np.cos, np.sin))

    own_head = np.zeros((2, 3, 2, PAIRS, L // 2), np.uint32)
    own_head[0, :, 0] = own_head[1, :, 1] = 0x3F803F80
    own_head = own_head.view(np.float32).reshape(MROWS, H, L // 2)

    def lay(a, *axes):
        return np.ascontiguousarray(np.transpose(np.asarray(a), axes))

    def by_dimension(w):
        return lay(np.asarray(w).reshape(PAIRS, 2, HD, D), 3, 1, 2, 0).reshape(D, D)

    arrays = dict(x=np.ascontiguousarray(L0_attn_x), w_q=by_dimension(L0_attn_W_Q), w_k=by_dimension(L0_attn_W_K),
                  w_v=lay(L0_attn_W_V, 1, 0), w_o=lay(L0_attn_W_O, 1, 0), w_g=lay(L0_ffn_Wg, 1, 0),
                  w1=lay(L0_ffn_W1, 2, 0, 1), w2=lay(L0_ffn_W2, 2, 0, 1), w3=lay(L0_ffn_W3, 2, 0, 1),
                  cos_t=cos_t, sin_t=sin_t, own_head=own_head)
    nc = bacc.Bacc("TRN2", target_bir_lowering=False, num_devices=1)
    args = [nc.dram_tensor(f"in_{n}", arrays[n].shape, F32, kind="ExternalInput").ap() for n in INS]
    out = nc.dram_tensor("out", (B, L, D), F32, kind="ExternalOutput").ap()
    block_kernel(nc, *args, out)
    r = run_bass_kernel_spmd(nc, [{f"in_{n}": arrays[n] for n in INS}], core_ids=[0])
    return r.results[0]["out"]
```
